# Optimizing a Trainium2 kernel written in Bass

```python
import numpy as np
import jax
import jax.numpy as jnp

def _softmax(x, axis=-1):
    return jax.nn.softmax(x, axis=axis)

def _gelu(x):
    return jax.nn.gelu(x, approximate=True)

def _silu(x):
    return jax.nn.silu(x)

def _sigmoid(x):
    return jax.nn.sigmoid(x)

def _layernorm(x, axis=-1, eps=1e-05):
    m = jnp.mean(x, axis=axis, keepdims=True)
    v = jnp.var(x, axis=axis, keepdims=True)
    return (x - m) / jnp.sqrt(v + eps)

def _scatter_add(tgt, idx, src, axis=0):
    return tgt.at[idx].add(src)

def _segment_sum(src, seg, n):
    return jax.ops.segment_sum(src, seg, n)
kernel_name = 'mk_macaron_d2_jaxref_r8_ffef19'

def setup_inputs(seed: int=0):
    np.random.seed(seed)
    _w = jnp.asarray

    def _L0_attn_setup():
        import jax, jax.numpy as jnp
        import numpy as np
        BLOCK_H = 32
        BLOCK_W = 32
        N_FEAT = 512
        K_FEAT = 512
        key = jax.random.key(seed)
        k1, k2, k3 = jax.random.split(key, 3)
        data = jax.random.normal(k1, (4, 128, K_FEAT), dtype=jnp.float32)
        weight = jax.random.normal(k2, (N_FEAT, K_FEAT), dtype=jnp.float32) * 0.02
        nb, kb = (N_FEAT // BLOCK_H, K_FEAT // BLOCK_W)
        block_pattern = jax.random.randint(k3, (nb, kb), 0, 2, dtype=jnp.int32)
        mask = jnp.repeat(jnp.repeat(block_pattern, BLOCK_H, axis=0), BLOCK_W, axis=1)
        return {'data': data, 'weight': weight, 'mask': mask}
    _L0_attn_in = _L0_attn_setup()

    def _L0_ffn_setup():
        import jax, jax.numpy as jnp
        import numpy as np
        key = jax.random.key(seed)
        k = jax.random.split(key, 6)
        x = jax.random.normal(k[0], (4, 256, 512), jnp.float32)
        W = jax.random.normal(k[1], (512, 512), jnp.float32) * 0.02
        bias = jax.random.normal(k[2], (512,), jnp.float32) * 0.02
        A = jax.random.normal(k[3], (16, 16, 512), jnp.float32) * 0.02
        Bf = jax.random.normal(k[4], (16, 512, 16), jnp.float32) * 0.02
        coeffs = jax.random.uniform(k[5], (16,), jnp.float32)
        scales = jnp.full((16,), 0.5, jnp.float32)
        return {'x': x, 'W': W, 'bias': bias, 'A': A, 'Bf': Bf, 'coeffs': coeffs, 'scales': scales}
    _L0_ffn_in = _L0_ffn_setup()

    def _L1_attn_setup():
        import jax, jax.numpy as jnp
        import numpy as np
        D_MODEL, N_HEADS, LATENT, ROPE = (512, 128, 64, 64)
        HEAD_DIM = D_MODEL // N_HEADS
        B, S = (2, 128)
        key = jax.random.key(seed)
        ks = jax.random.split(key, 9)

        def w(k, i, o):
            return jax.random.normal(k, (i, o), dtype=jnp.float32) * (1.0 / np.sqrt(i))
        return {'x': jax.random.normal(ks[0], (B, S, D_MODEL), dtype=jnp.float32), 'Wq_down': w(ks[1], D_MODEL, LATENT), 'Wq_up': w(ks[2], LATENT, N_HEADS * HEAD_DIM), 'Wq_rope': w(ks[3], D_MODEL, N_HEADS * ROPE), 'Wkv_down': w(ks[4], D_MODEL, LATENT), 'Wk_up': w(ks[5], LATENT, N_HEADS * HEAD_DIM), 'Wv_up': w(ks[6], LATENT, N_HEADS * HEAD_DIM), 'Wk_rope': w(ks[7], D_MODEL, ROPE), 'Wo': w(ks[8], N_HEADS * HEAD_DIM, D_MODEL)}
    _L1_attn_in = _L1_attn_setup()

    def _L1_ffn_setup():
        import jax, jax.numpy as jnp
        import numpy as np
        H = 512
        I = 1376
        B, S = (2, 256)
        key = jax.random.key(seed)
        k1, k2, k3 = jax.random.split(key, 3)
        x = jax.random.normal(k1, (B, S, H), dtype=jnp.float32)
        w_gate_up = jax.random.normal(k2, (2 * I, H), dtype=jnp.float32) * 0.02
        w_down = jax.random.normal(k3, (H, I), dtype=jnp.float32) * 0.02
        return {'x': x, 'w_gate_up': w_gate_up, 'w_down': w_down}
    _L1_ffn_in = _L1_ffn_setup()
    _d = {'L0_attn_data': _L0_attn_in['data'], 'L0_attn_weight': _L0_attn_in['weight'], 'L0_attn_mask': _L0_attn_in['mask'], 'L0_ffn_W': _L0_ffn_in['W'], 'L0_ffn_bias': _L0_ffn_in['bias'], 'L0_ffn_A': _L0_ffn_in['A'], 'L0_ffn_Bf': _L0_ffn_in['Bf'], 'L0_ffn_coeffs': _L0_ffn_in['coeffs'], 'L0_ffn_scales': _L0_ffn_in['scales'], 'L1_attn_Wq_down': _L1_attn_in['Wq_down'], 'L1_attn_Wq_up': _L1_attn_in['Wq_up'], 'L1_attn_Wq_rope': _L1_attn_in['Wq_rope'], 'L1_attn_Wkv_down': _L1_attn_in['Wkv_down'], 'L1_attn_Wk_up': _L1_attn_in['Wk_up'], 'L1_attn_Wv_up': _L1_attn_in['Wv_up'], 'L1_attn_Wk_rope': _L1_attn_in['Wk_rope'], 'L1_attn_Wo': _L1_attn_in['Wo'], 'L1_ffn_w_gate_up': _L1_ffn_in['w_gate_up'], 'L1_ffn_w_down': _L1_ffn_in['w_down']}
    _x0 = _d['L0_attn_data']
    _d['L0_attn_data'] = jax.random.normal(jax.random.fold_in(jax.random.key(seed), 1), (8, 256, 512), dtype=_x0.dtype)
    del _x0
    return _d

def reference(L0_attn_data, L0_attn_weight, L0_attn_mask, L0_ffn_W, L0_ffn_bias, L0_ffn_A, L0_ffn_Bf, L0_ffn_coeffs, L0_ffn_scales, L1_attn_Wq_down, L1_attn_Wq_up, L1_attn_Wq_rope, L1_attn_Wkv_down, L1_attn_Wk_up, L1_attn_Wv_up, L1_attn_Wk_rope, L1_attn_Wo, L1_ffn_w_gate_up, L1_ffn_w_down):

    def _L0_attn_ref(data, weight, mask):
        import jax, jax.numpy as jnp
        import numpy as np
        BLOCK_H = 32
        BLOCK_W = 32
        N_FEAT = 512
        K_FEAT = 512
        N, K = weight.shape
        nb, kb = (N // BLOCK_H, K // BLOCK_W)
        block_mask = mask.reshape(nb, BLOCK_H, kb, BLOCK_W).astype(jnp.float32).sum(axis=(1, 3)) > 0
        elem_mask = jnp.repeat(jnp.repeat(block_mask, BLOCK_H, axis=0), BLOCK_W, axis=1)
        w_masked = weight * elem_mask.astype(weight.dtype)
        out = jnp.einsum('bsk,nk->bsn', data, w_masked)
        return out

    def _L0_ffn_ref(x, W, bias, A, Bf, coeffs, scales):
        import jax, jax.numpy as jnp
        import numpy as np
        out = jnp.einsum('bsd,od->bso', x, W) + bias
        xa = jnp.einsum('bsd,erd->ebsr', x, A)
        w = coeffs * scales
        upd = jnp.einsum('ebsr,eor,e->bso', xa, Bf, w)
        return out + upd

    def _L1_attn_ref(x, Wq_down, Wq_up, Wq_rope, Wkv_down, Wk_up, Wv_up, Wk_rope, Wo):
        import jax, jax.numpy as jnp
        import numpy as np
        D_MODEL, N_HEADS, LATENT, ROPE = (512, 128, 64, 64)
        HEAD_DIM = D_MODEL // N_HEADS
        B, S = (2, 128)
        b, s, _ = x.shape
        c_q = x @ Wq_down
        c_kv = x @ Wkv_down
        q_c = (c_q @ Wq_up).reshape(b, s, N_HEADS, HEAD_DIM)
        q_r = (x @ Wq_rope).reshape(b, s, N_HEADS, ROPE)
        k_c = (c_kv @ Wk_up).reshape(b, s, N_HEADS, HEAD_DIM)
        v_c = (c_kv @ Wv_up).reshape(b, s, N_HEADS, HEAD_DIM)
        k_r = x @ Wk_rope
        scale = jnp.asarray((HEAD_DIM + ROPE) ** 0.5, x.dtype)
        scores = (jnp.einsum('bqhd,bkhd->bhqk', q_c, k_c) + jnp.einsum('bqhd,bkd->bhqk', q_r, k_r)) / scale
        attn = jax.nn.softmax(scores, axis=-1)
        out = jnp.einsum('bhqk,bkhd->bqhd', attn, v_c)
        out = out.reshape(b, s, N_HEADS * HEAD_DIM)
        return out @ Wo

    def _L1_ffn_ref(x, w_gate_up, w_down):
        import jax, jax.numpy as jnp
        import numpy as np
        H = 512
        I = 1376
        B, S = (2, 256)
        gate_up = jnp.einsum('bsh,oh->bso', x, w_gate_up)
        d = gate_up.shape[-1] // 2
        h = jax.nn.silu(gate_up[..., :d]) * gate_up[..., d:]
        return jnp.einsum('bsi,hi->bsh', h, w_down)
    x = L0_attn_data
    x = x + 0.5 * _L0_ffn_ref(_layernorm(x, axis=-1), L0_ffn_W, L0_ffn_bias, L0_ffn_A, L0_ffn_Bf, L0_ffn_coeffs, L0_ffn_scales)
    x = x + _L0_attn_ref(_layernorm(x, axis=-1), L0_attn_weight, L0_attn_mask)
    x = x + 0.5 * _L0_ffn_ref(_layernorm(x, axis=-1), L0_ffn_W, L0_ffn_bias, L0_ffn_A, L0_ffn_Bf, L0_ffn_coeffs, L0_ffn_scales)
    x = x + 0.5 * _L1_ffn_ref(_layernorm(x, axis=-1), L1_ffn_w_gate_up, L1_ffn_w_down)
    x = x + _L1_attn_ref(_layernorm(x, axis=-1), L1_attn_Wq_down, L1_attn_Wq_up, L1_attn_Wq_rope, L1_attn_Wkv_down, L1_attn_Wk_up, L1_attn_Wv_up, L1_attn_Wk_rope, L1_attn_Wo)
    x = x + 0.5 * _L1_ffn_ref(_layernorm(x, axis=-1), L1_ffn_w_gate_up, L1_ffn_w_down)
    return x

_drawn_inputs = setup_inputs


def setup_inputs(seed=0):
    import zlib

    import numpy as np

    out = dict(_drawn_inputs(seed))
    spreads = {'L0_ffn_scales': (0.5, 0.6)}
    factors = {'L0_ffn_coeffs': 3.917, 'L0_ffn_bias': 2.672}
    for name, (base, spread) in spreads.items():
        noise = np.random.default_rng([zlib.crc32(name.encode()), seed]).standard_normal(out[name].shape)
        drawn = base * np.exp(spread * noise) if base else spread * noise
        out[name] = jnp.asarray(drawn.astype(out[name].dtype))
    for name, factor in factors.items():
        out[name] = (out[name] * factor).astype(out[name].dtype)
    return out
```

```python
import concourse.bass as bass
from concourse import mybir
from contextlib import ExitStack

F32 = mybir.dt.float32
F32R = mybir.dt.float32r
I32 = mybir.dt.int32
ALU = mybir.AluOpType
ACT = mybir.ActivationFunctionType
AXX = mybir.AxisListType.X

P = 128
TOK, D = 2048, 512
NT = TOK // P
G = 4
GT = NT // G
GW = GT * P
DC = D // P
S = 256
ER = 256
MB = 32
I_FF = 1376
NI = -(-I_FF // P)
CW = 3 * D
L0_AT = 8 * CW
H = 128
HD, ROPE = 4, 64
NHP = H // 2
UNITS = NHP * G
SC = float(HD + ROPE) ** -0.5
EX = 3 * HD
KM = ROPE + HD
KROW = ROPE + EX
EPS = 1e-5


def split_products(nc, out, hi_w, lo_w, hi_x, lo_x, first, last):
    nc.tensor.matmul(out, hi_w, hi_x, start=first, stop=False)
    nc.tensor.matmul(out, lo_w, hi_x, start=False, stop=False)
    return nc.tensor.matmul(out, hi_w, lo_x, start=False, stop=last)


def build(nc, x, wT, mwT, maskT, a_er, b_er, coef, scal, bias, ffw, wdown, wqu, wku, wvu, wrope, wo, out):
    ctx = ExitStack()
    with ctx:
        def sem(name):
            return ctx.enter_context(nc.semaphore(name))

        def sbuf(stack, name, shape, dt):
            return stack.enter_context(nc.sbuf_tensor(name, shape, dt))

        x_mid = nc.dram_tensor("x_mid", (NT, P, D), F32).ap()
        exq = nc.dram_tensor("exq", (H, EX, TOK), F32).ap()
        exk = nc.dram_tensor("exk", (H, EX, TOK), F32).ap()
        att = nc.dram_tensor("att", (2, D, TOK), F32).ap()

        psum = ctx.enter_context(nc.psum_tensor("psum", [P, 8 * 512], F32))

        def bank(n):
            return psum[:, 512 * n:512 * n + 512]

        ident = sbuf(ctx, "ident", [P, P], F32)
        stat = sbuf(ctx, "stat", [P, GT, 6], F32)
        mv = sbuf(ctx, "mv", [P, GT, 2], F32)
        rstd = sbuf(ctx, "rstd", [P, GT], F32)
        nbias = sbuf(ctx, "nbias", [P, GT], F32)
        veps = sbuf(ctx, "veps", [P, GT], F32)
        minus_half = sbuf(ctx, "minus_half", [P, GT], F32)

        set_a = ExitStack()
        X = sbuf(set_a, "X", [P, NT, D], F32)
        WH = sbuf(set_a, "WH", [P, NI * CW], F32R)
        WL = sbuf(set_a, "WL", [P, NI * CW], F32R)
        bias_half = sbuf(set_a, "bias_half", [P, D], F32)
        setup = ExitStack()
        s_wT = sbuf(setup, "s_wT", [P, DC * D], F32)
        s_mw = sbuf(setup, "s_mw", [P, DC * D], F32)
        s_mask = sbuf(setup, "s_mask", [P, DC * D], I32)
        s_a = sbuf(setup, "s_a", [P, 2, D], F32)
        s_b = sbuf(setup, "s_b", [P, 2, D], F32)
        s_coef = sbuf(setup, "s_coef", [P, 2], F32)
        s_scal = sbuf(setup, "s_scal", [P, 2], F32)
        s_bias = sbuf(setup, "s_bias", [1, D], F32)
        s_ones = sbuf(setup, "s_ones", [1, P], F32)
        s_bd = sbuf(setup, "s_bd", [P, P], F32)
        s_cnt = sbuf(setup, "s_cnt", [P, DC * D // MB], F32)
        s_keep = sbuf(setup, "s_keep", [P, DC * D // MB], F32)
        setup.close()
        XTH = sbuf(set_a, "XTH", [P, DC, GW], F32R)
        XTL = sbuf(set_a, "XTL", [P, DC, GW], F32R)
        HH = sbuf(set_a, "HH", [P, 2, GW], F32R)
        HL = sbuf(set_a, "HL", [P, 2, GW], F32R)
        XN = sbuf(set_a, "XN", [P, 2, D], F32)
        RAW = sbuf(set_a, "RAW", [P, CW], F32)
        SG = sbuf(set_a, "SG", [P, GW], F32)
        HF = sbuf(set_a, "HF", [P, GW], F32)
        set_a.close()

        set_b = ExitStack()
        XAH = sbuf(set_b, "XAH", [P, DC, TOK], F32R)
        XAL = sbuf(set_b, "XAL", [P, DC, TOK], F32R)
        K1 = sbuf(set_b, "K1", [P, 2, TOK], F32R)
        K2 = sbuf(set_b, "K2", [P, TOK], F32R)
        X1 = sbuf(set_b, "X1", [P, G, 2, GW], F32R)
        X2 = sbuf(set_b, "X2", [P, G, 2, GW], F32R)
        WRH = sbuf(set_b, "WRH", [P, 2, DC * P], F32R)
        WRL = sbuf(set_b, "WRL", [P, 2, DC * P], F32R)
        NM = sbuf(set_b, "NM", [8, 2, P], F32R)
        PB = sbuf(set_b, "PB", [P, 2, 4 * 512], F32)
        WRAW = sbuf(set_b, "WRAW", [P, 2, DC * P], F32)
        VST = sbuf(set_b, "VST", [P, NT, 2, 32], F32)
        VA = sbuf(set_b, "VA", [P, NT, D], F32)
        OSB = sbuf(set_b, "OSB", [P, G, S], F32)
        WUP = sbuf(set_b, "WUP", [P, 2, D], F32)
        MXS = sbuf(set_b, "MXS", [P, 2, 8], F32)
        b_x = PB[:, :, :].rearrange("p a (t d) -> p a t d", t=GT)
        b_xn = WRAW
        b_wd = VST[:, :, :, :].rearrange("p a b c -> p (a b c)")
        b_wdh = WRH[:, :, :].rearrange("p a (b n) -> p (a b) n", n=2 * P)
        b_wdl = WRL[:, :, :].rearrange("p a (b n) -> p (a b) n", n=2 * P)
        b_c = OSB[:, 0:2, :].rearrange("p a b -> p (a b)")
        b_kt = X2[:, 0, 0, :]
        b_eh = X2[:, 1, :, :]
        b_el = X2[:, 2, :, :]
        set_b.close()

        x_loaded, setup_loaded, setup_done = sem("x_loaded"), sem("setup_loaded"), sem("setup_done")
        wts = dict((n, sem(n)) for n in ("w_ready", "b_ready", "cnt_ready", "cnt_sum", "keep_ready", "upd_done",
                                         "weff_done", "mw_done", "wh_done", "bias_bc", "ident0", "ident_done",
                                         "consts_done"))

        def half(W, n):
            return W[:, L0_AT + n * DC * D:L0_AT + (n + 1) * DC * D]

        with nc.Block() as block:
            @block.sync
            def _(sp):
                for dst, src in ((s_coef[:, :], coef), (s_scal[:, :], scal), (s_b[:, :, :], b_er),
                                 (s_a[:, :, :], a_er), (s_wT[:, :], wT), (s_bias[:, :], bias),
                                 (s_mask[:, :], maskT), (s_mw[:, :], mwT)):
                    sp.dma_start(dst, src).then_inc(setup_loaded, 16)
                for g in range(G):
                    sp.dma_start(X[:, GT * g:GT * (g + 1), :],
                                 x[GT * g:GT * (g + 1)].rearrange("t p d -> p t d")).then_inc(x_loaded, 16)

            @block.gpsimd
            def _(pool):
                nc.gpsimd.memset(ident[:, :], 0.0).then_inc(wts["ident0"], 1)
                pool.wait_ge(wts["ident0"], 1)
                nc.gpsimd.affine_select(out=ident[:, :], in_=ident[:, :], compare_op=ALU.not_equal, fill=1.0, base=0,
                                        pattern=[[-1, P]], channel_multiplier=1).then_inc(wts["ident_done"], 1)

            @block.vector
            def _(dve):
                nc.vector.memset(s_bd[:, :], 0.0).then_inc(wts["consts_done"], 1)
                nc.vector.memset(s_ones[:, :], 1.0).then_inc(wts["consts_done"], 1)
                dve.wait_ge(wts["consts_done"], 2)
                for n in range(P // MB):
                    nc.vector.memset(s_bd[MB * n:MB * (n + 1), MB * n:MB * (n + 1)], 1.0).then_inc(wts["consts_done"], 1)
                dve.wait_ge(setup_loaded, 8 * 16)
                nc.vector.tensor_tensor(s_coef[:, :], s_coef[:, :], s_scal[:, :], ALU.mult).then_inc(wts["w_ready"], 1)
                dve.wait_ge(wts["w_ready"], 1)
                for k in range(2):
                    nc.vector.tensor_scalar(s_b[:, k, :], s_b[:, k, :], s_coef[:, k:k + 1], None,
                                            ALU.mult).then_inc(wts["b_ready"], 1)
                nc.vector.tensor_reduce(s_cnt[:, :], s_mask[:, :].rearrange("p (n m) -> p n m", m=MB), AXX,
                                        ALU.add).then_inc(wts["cnt_ready"], 1)
                dve.wait_ge(wts["bias_bc"], 1)
                nc.vector.tensor_scalar(bias_half[:, :], bank(5), 0.5, None, ALU.mult).then_inc(setup_done, 1)
                dve.wait_ge(wts["cnt_sum"], 1)
                nc.vector.tensor_scalar(s_keep[:, :], bank(4)[:, 0:DC * D // MB], 0.0, None,
                                        ALU.is_gt).then_inc(wts["keep_ready"], 1)
                dve.wait_ge(wts["keep_ready"], 1)
                m3 = s_mw[:, :].rearrange("p (n m) -> p n m", m=MB)
                nc.vector.tensor_tensor(m3, m3, s_keep[:, :].unsqueeze(2).broadcast_to([P, DC * D // MB, MB]),
                                        ALU.mult).then_inc(wts["mw_done"], 1)
                for c in range(DC):
                    dve.wait_ge(wts["upd_done"], c + 1)
                    nc.vector.tensor_tensor(s_wT[:, D * c:D * (c + 1)], bank(c), s_wT[:, D * c:D * (c + 1)],
                                            ALU.add).then_inc(wts["weff_done"], 1)
                dve.wait_ge(wts["wh_done"], 1)
                nc.vector.tensor_tensor(half(WL, 1), s_mw[:, :], half(WH, 1), ALU.subtract).then_inc(setup_done, 1)
                dve.wait_ge(wts["wh_done"], 2)
                nc.vector.tensor_tensor(half(WL, 0), s_wT[:, :], half(WH, 0), ALU.subtract).then_inc(setup_done, 1)

            @block.scalar
            def _(act):
                act.wait_ge(wts["mw_done"], 1)
                nc.scalar.copy(half(WH, 1), s_mw[:, :]).then_inc(wts["wh_done"], 1)
                act.wait_ge(wts["weff_done"], DC)
                nc.scalar.copy(half(WH, 0), s_wT[:, :]).then_inc(wts["wh_done"], 1)

            @block.tensor
            def _(pe):
                pe.wait_ge(setup_loaded, 8 * 16)
                pe.wait_ge(wts["consts_done"], 2 + P // MB)
                nc.tensor.matmul(bank(5), s_ones[:, :], s_bias[:, :], start=True, stop=True).then_inc(wts["bias_bc"], 1)
                pe.wait_ge(wts["cnt_ready"], 1)
                nc.tensor.matmul(bank(4)[:, 0:DC * D // MB], s_bd[:, :], s_cnt[:, :], start=True,
                                 stop=True).then_inc(wts["cnt_sum"], 1)
                pe.wait_ge(wts["b_ready"], 2)
                for c in range(DC):
                    for k in range(2):
                        last = nc.tensor.matmul(bank(c), s_a[:, k, P * c:P * (c + 1)], s_b[:, k, :], start=(k == 0),
                                                stop=(k == 1))
                    last.then_inc(wts["upd_done"], 1)

        def dense_sems(tag):
            return dict((n, sem(tag + n)) for n in (
                "stat_step", "var", "rstd", "stats", "normed", "transposed", "high", "low", "products", "acc", "residual",
                "raw_loaded", "raw_high", "split", "gate_up", "gated", "hidden", "hidden_high", "hidden_low", "down",
                "stored", "loaded", "raw_read", "consts", "waited"))

        def tp_bank(t):
            return bank(4 + (t + 2) % 4)

        def group_stats(dve, s, n, srcs):
            for t in range(GT):
                nc.vector.bn_stats(stat[:, t, :], srcs[t]).then_inc(s["stat_step"], 1)
            dve.wait_ge(s["stat_step"], n * (2 * GT) + GT)
            dve.sem_inc(s["waited"], 1)
            for t in range(GT):
                nc.vector.bn_aggr(mv[:, t, :], stat[:, t, :]).then_inc(s["stat_step"], 1)
            dve.wait_ge(s["stat_step"], n * (2 * GT) + 2 * GT)
            nc.vector.tensor_scalar(veps[:, :], mv[:, :, 1], EPS, None, ALU.add).then_inc(s["var"], 1)
            dve.wait_ge(s["rstd"], n + 1)
            nc.vector.scalar_tensor_tensor(out=nbias[:, :], in0=mv[:, :, 0], scalar=-1.0, in1=rstd[:, :],
                                           op0=ALU.mult, op1=ALU.mult).then_inc(s["stats"], 1)

        def inverse_root(pool, s, n):
            pool.wait_ge(s["var"], n + 1)
            nc.gpsimd.tensor_tensor(rstd[:, :], veps[:, :], minus_half[:, :], ALU.pow).then_inc(s["rstd"], 1)

        def normalise(act, s, n, group, t, src, dst, wait_slot):
            act.wait_ge(s["stats"], group + 1)
            if wait_slot:
                act.wait_ge(s["transposed"], n - 1)
            nc.scalar.activation(dst, src, ACT.Identity, bias=nbias[:, t:t + 1],
                                 scale=rstd[:, t:t + 1]).then_inc(s["normed"], 1)

        def transpose(pe, s, n, t, src, wait_bank):
            pe.wait_ge(s["normed"], n + 1)
            if wait_bank is not None:
                pe.wait_ge(s["low"], wait_bank)
            for c in range(DC):
                last = nc.tensor.transpose(tp_bank(t)[:, P * c:P * (c + 1)], src[:, P * c:P * (c + 1)], ident[:, :])
            last.then_inc(s["transposed"], 1)

        def chunks(ap):
            return ap.rearrange("p (c n) -> p c n", c=DC)

        def high_half(act, s, n, t, dst):
            act.wait_ge(s["transposed"], n + 1)
            nc.scalar.copy(dst, chunks(tp_bank(t))).then_inc(s["high"], 1)

        def low_half(dve, s, m, t, dst, high):
            dve.wait_ge(s["high"], m + 1)
            nc.vector.tensor_tensor(dst, chunks(tp_bank(t)), high, ALU.subtract).then_inc(s["low"], 1)

        def xt(W, t):
            return W[:, :, P * t:P * (t + 1)]

        def xtile(T):
            return X[:, bass.ds(T, 1), :].rearrange("p a d -> p (a d)")

        def linear_pe(pe, s, m, w):
            def product(t):
                pe.wait_ge(s["low"], m + (t + 1))
                if not isinstance(m, int) or m + t >= 4:
                    pe.wait_ge(s["residual"], m + (t - 3))
                for c in range(DC):
                    wh, wl = (half(W, w)[:, D * c:D * (c + 1)] for W in (WH, WL))
                    last = split_products(nc, bank(t), XTH[:, c, P * t:P * (t + 1)], XTL[:, c, P * t:P * (t + 1)], wh,
                                          wl, c == 0, c == DC - 1)
                last.then_inc(s["products"], 1)

            product(0)
            for t in range(GT):
                if t + 1 < GT:
                    product(t + 1)
                transpose(pe, s, m + (t + 4), t, XN[:, t % 2, :], m + (t + 1))

        def linear_act(act, s, m, n, T_next):
            for t in range(GT):
                normalise(act, s, m + (t + 4), n + 1, t, xtile(T_next + t), XN[:, t % 2, :], True)
                if t > 0:
                    high_half(act, s, m + (t + 3), t - 1, xt(XTH, t - 1))
            high_half(act, s, m + (GT + 3), GT - 1, xt(XTH, GT - 1))

        def linear_dve(dve, s, m, n, T, T_next, first_stage, bias_at):
            if not first_stage:
                dve.wait_ge(s["residual"], m + (2 * GT - NT))
            dve.wait_ge(s["normed"], m + GT)
            group_stats(dve, s, n + 1, [xtile(T_next + t) for t in range(GT)])
            for t in range(GT):
                dve.wait_ge(s["products"], m + (t + 1))
                if bias_at is None:
                    residual(s, t, T, 1.0, s["residual"])
                else:
                    residual(s, t, T, 0.5, s["acc"])
                    dve.wait_ge(s["acc"], bias_at + (t + 1))
                    nc.vector.tensor_tensor(xtile(T + t), xtile(T + t), bias_half[:, :],
                                            ALU.add).then_inc(s["residual"], 1)
                if t > 0:
                    low_half(dve, s, m + (t + 3), t - 1, xt(XTL, t - 1), xt(XTH, t - 1))
            low_half(dve, s, m + (GT + 3), GT - 1, xt(XTL, GT - 1), xt(XTH, GT - 1))

        def residual(s, t, T, factor, signal):
            nc.vector.scalar_tensor_tensor(out=xtile(T + t), in0=bank(t), scalar=factor, in1=xtile(T + t),
                                           op0=ALU.mult, op1=ALU.add).then_inc(signal, 1)

        def gate_up(pe, s, m, g, i):
            if i == 0:
                pe.wait_ge(s["low"], m + GT)
            elif i >= 2:
                pe.wait_ge(s["hidden"], g * NI + (i - 1))
            pe.wait_ge(s["split"], i + 1)
            for k in range(2):
                for c in range(DC):
                    a = i * CW + k * D + c * P
                    last = split_products(nc, bank(4 + 2 * (i % 2) + k), WH[:, a:a + P], WL[:, a:a + P], XTH[:, c, :],
                                          XTL[:, c, :], c == 0, c == DC - 1)
            last.then_inc(s["gate_up"], 1)

        def down(pe, s, m, g, i, wait_banks):
            pe.wait_ge(s["hidden_low"], g * NI + (i + 1))
            if i == 0 and wait_banks:
                pe.wait_ge(s["residual"], m)
            a = i * CW + 2 * D
            for t in range(GT):
                hh, hl = (W[:, i % 2, P * t:P * (t + 1)] for W in (HH, HL))
                last = split_products(nc, bank(t), hh, hl, WH[:, a:a + D], WL[:, a:a + D], i == 0, i == NI - 1)
                if i == NI - 1:
                    last.then_inc(s["products"], 1)
            if i < NI - 1:
                last.then_inc(s["down"], 1)

        def ffn_pe(pe, s, m, g, ln, ahead):
            for i in range(NI):
                gate_up(pe, s, m, g, i)
                if i > 0:
                    down(pe, s, m, g, i - 1, True)
            if ahead:
                for t in (0, 1):
                    transpose(pe, s, ln + t, t, XN[:, t % 2, :], None)
            down(pe, s, m, g, NI - 1, True)
            if ahead:
                for t in (2, 3):
                    transpose(pe, s, ln + t, t, XN[:, t % 2, :], None)

        def ffn_act(act, s, m, g, ln, n, T_next, ahead):
            for i in range(NI):
                b = bank(4 + 2 * (i % 2))
                act.wait_ge(s["gate_up"], g * NI + (i + 1))
                if i > 0:
                    act.wait_ge(s["hidden"], g * NI + i)
                nc.scalar.activation(SG[:, :], b, ACT.Silu).then_inc(s["gated"], 1)
                act.wait_ge(s["hidden"], g * NI + (i + 1))
                if i >= 2:
                    act.wait_ge(s["down"], g * (NI - 1) + (i - 1))
                nc.scalar.copy(HH[:, i % 2, :], HF[:, :]).then_inc(s["hidden_high"], 1)
                if ahead and i == 8:
                    for t in (0, 1):
                        normalise(act, s, ln + t, n, t, xtile(T_next + t), XN[:, t % 2, :], True)
            if ahead:
                for t in range(GT):
                    high_half(act, s, ln + t, t, xt(XTH, t))
                    if t < 2:
                        normalise(act, s, ln + (t + 2), n, t + 2, xtile(T_next + (t + 2)), XN[:, t % 2, :], True)

        def ffn_dve(dve, s, m, g, ln, n, T, T_next, ahead, prior):
            for i in range(NI):
                dve.wait_ge(s["gated"], g * NI + (i + 1))
                if i > 0:
                    dve.wait_ge(s["hidden_low"], g * NI + i)
                nc.vector.tensor_tensor(HF[:, :], bank(5 + 2 * (i % 2)), SG[:, :], ALU.mult).then_inc(s["hidden"], 1)
                if ahead and i == 4:
                    dve.wait_ge(s["residual"], prior)
                    dve.wait_ge(s["normed"], ln)
                    group_stats(dve, s, n, [xtile(T_next + t) for t in range(GT)])
                dve.wait_ge(s["hidden_high"], g * NI + (i + 1))
                if i >= 2:
                    dve.wait_ge(s["down"], g * (NI - 1) + (i - 1))
                nc.vector.tensor_tensor(HL[:, i % 2, :], HF[:, :], HH[:, i % 2, :],
                                        ALU.subtract).then_inc(s["hidden_low"], 1)
            order = [("low", 0), ("low", 1), ("res", 0), ("res", 1), ("res", 2), ("low", 2), ("low", 3), ("res", 3)]
            for what, t in order:
                if what == "low" and ahead:
                    low_half(dve, s, m + (t + 4), t, xt(XTL, t), xt(XTH, t))
                elif what == "res":
                    dve.wait_ge(s["products"], m + (t + 1))
                    residual(s, t, T, 0.5, s["residual"])

        def load_chunks(sp, s, before):
            for i in range(NI):
                if before + i > 0:
                    sp.wait_ge(s["raw_read"], before + i)
                sp.dma_start(RAW[:, :], ffw[i]).then_inc(s["raw_loaded"], 16)

        def split_piece(pool, s, n, a, width, signal_split):
            pool.wait_ge(s["raw_loaded"], 16 * (n + 1))
            nc.gpsimd.tensor_scalar(WH[:, a:a + width], RAW[:, 0:width], 1.0, 1.0, ALU.mult,
                                    ALU.mult).then_inc(s["raw_high"], 1)
            pool.wait_ge(s["raw_high"], n + 1)
            low = nc.gpsimd.tensor_tensor(WL[:, a:a + width], RAW[:, 0:width], WH[:, a:a + width], ALU.subtract)
            low.then_inc(s["raw_read"], 1)
            if signal_split:
                pool.wait_ge(s["raw_read"], n + 1)
                pool.sem_inc(s["split"], 1)

        sa = dense_sems("a_")
        LAYERS = (0, 1, 0)
        FF0 = len(LAYERS) * NT
        LG = len(LAYERS) * G

        with nc.Block() as block:
            @block.sync
            def _(sp):
                load_chunks(sp, sa, 0)
                for g in range(G):
                    sp.wait_ge(sa["residual"], FF0 + GT * (g + 1))
                    sp.dma_start(x_mid[GT * g:GT * (g + 1)].rearrange("t p d -> p t d"),
                                 X[:, GT * g:GT * (g + 1), :]).then_inc(sa["stored"], 16)
                sp.wait_ge(sa["stored"], 16 * G)

            @block.gpsimd
            def _(pool):
                inverse_root(pool, sa, 0)
                for n in range(LG):
                    inverse_root(pool, sa, n + 1)
                    if n * CW < L0_AT:
                        split_piece(pool, sa, n, n * CW, CW, True)
                pool.wait_ge(sa["products"], FF0)
                for i in range(L0_AT // CW, NI):
                    split_piece(pool, sa, i, i * CW, CW, True)
                for n in range(LG + 1, LG + G):
                    inverse_root(pool, sa, n)

            @block.tensor
            def _(pe):
                for t in range(GT):
                    transpose(pe, sa, t, t, XN[:, t % 2, :], None)
                for layer, w in enumerate(LAYERS):
                    m0 = layer * NT
                    if layer == 0:
                        linear_pe(pe, sa, 0, w)
                    with pe.Fori(int(layer == 0), G) as g:
                        linear_pe(pe, sa, g * GT + m0, w)
                with pe.Fori(0, G - 1) as g:
                    ffn_pe(pe, sa, g * GT + FF0, g, g * GT + (FF0 + GT), True)
                ffn_pe(pe, sa, FF0 + NT - GT, G - 1, 0, False)

            @block.scalar
            def _(act):
                for t in range(GT):
                    normalise(act, sa, t, 0, t, X[:, t, :], XN[:, t % 2, :], t >= 2)
                    high_half(act, sa, t, t, xt(XTH, t))
                for layer, w in enumerate(LAYERS):
                    m0 = layer * NT
                    with act.Fori(0, G - 1) as g:
                        linear_act(act, sa, g * GT + m0, g + G * layer, g * GT + GT)
                    linear_act(act, sa, m0 + NT - GT, G * layer + G - 1, 0)
                with act.Fori(0, G - 1) as g:
                    ffn_act(act, sa, g * GT + FF0, g, g * GT + (FF0 + GT), g + (LG + 1), g * GT + GT, True)
                ffn_act(act, sa, FF0 + NT - GT, G - 1, 0, 0, 0, False)

            @block.vector
            def _(dve):
                dve.wait_ge(setup_done, 3)
                dve.wait_ge(x_loaded, 16 * G)
                nc.vector.memset(minus_half[:, :], -0.5).then_inc(sa["consts"], 1)
                dve.wait_ge(sa["consts"], 1)
                group_stats(dve, sa, 0, [X[:, t, :] for t in range(GT)])
                for t in range(GT):
                    low_half(dve, sa, t, t, xt(XTL, t), xt(XTH, t))
                for layer, w in enumerate(LAYERS):
                    m0 = layer * NT
                    bias_at = None if w else (layer // 2) * NT
                    with dve.Fori(0, G - 1) as g:
                        linear_dve(dve, sa, g * GT + m0, g + G * layer, g * GT, g * GT + GT, layer == 0,
                                   None if bias_at is None else g * GT + bias_at)
                    linear_dve(dve, sa, m0 + NT - GT, G * layer + G - 1, NT - GT, 0, False,
                               None if bias_at is None else bias_at + NT - GT)
                with dve.Fori(0, G - 1) as g:
                    ffn_dve(dve, sa, g * GT + FF0, g, g * GT + (FF0 + GT), g + (LG + 1), g * GT, g * GT + GT, True,
                            g * GT + (FF0 + 2 * GT - NT))
                ffn_dve(dve, sa, FF0 + NT - GT, G - 1, 0, 0, NT - GT, 0, False, 0)

        sb = dense_sems("b_")
        sp1 = dict((n, sem("p_" + n)) for n in ("w_loaded", "wd_high", "wd_low", "c_ps", "k_ps", "c_sb", "k_high",
                                                "k_low", "ex_ps", "ex_high", "ex_low", "v_copied"))
        x_in = [sem(f"x_in{n}") for n in range(2)]
        ex_stored = [sem(f"ex_stored{n}") for n in range(2)]
        NEX = 2 * DC
        NOUT = NEX + GT

        with nc.Block() as block:
            @block.gpsimd
            def _(pool):
                for g in range(G):
                    inverse_root(pool, sb, g)

            @block.sync
            def _(sp):
                for dst, src in ((b_wd, wdown), (WUP[0:ROPE, 0, :], wqu), (WUP[ROPE:P, 0, :], wku),
                                 (WUP[ROPE:P, 1, :], wvu)):
                    sp.dma_start(dst, src).then_inc(sp1["w_loaded"], 16)

                def load_x(g):
                    if g >= 2:
                        sp.wait_ge(sb["normed"], GT * (g - 1))
                    sp.dma_start(b_x[:, g % 2, :, :], x_mid[GT * g:GT * (g + 1)].rearrange("t p d -> p t d")
                                 ).then_inc(x_in[g % 2], 16)

                load_x(0)
                load_x(1)
                for g in range(G):
                    if g + 2 < G:
                        load_x(g + 2)
                    for n in range(NEX):
                        c, eh, el = n % DC, b_eh[:, n % 2, :], b_el[:, n % 2, :]
                        ex, rows = (exq, ((0, eh), (1, eh), (2, el))) if n < DC else (exk, ((0, eh), (1, el), (2, eh)))
                        sp.wait_ge(sp1["ex_low"], NEX * g + n + 1)
                        for r, src in rows:
                            sp.dma_start(ex[32 * c:32 * (c + 1), HD * r:HD * (r + 1), GW * g:GW * (g + 1)],
                                         src.bitcast(F32)).then_inc(ex_stored[n % 2], 16)
                for n in range(2):
                    sp.wait_ge(ex_stored[n], 16 * 3 * NEX * G // 2)

            @block.vector
            def _(dve):
                def x_stats(g):
                    dve.wait_ge(x_in[g % 2], 16 * (g // 2 + 1))
                    if g > 0:
                        dve.wait_ge(sb["normed"], GT * g)
                    group_stats(dve, sb, g, [b_x[:, g % 2, t, :] for t in range(GT)])

                dve.wait_ge(sp1["wd_high"], 1)
                nc.vector.tensor_tensor(b_wdl, b_wd.rearrange("p (c n) -> p c n", c=DC), b_wdh,
                                        ALU.subtract).then_inc(sp1["wd_low"], 1)
                for g in range(G):
                    if g == 0:
                        x_stats(0)
                    for n in range(GT * g, GT * (g + 1)):
                        low_half(dve, sb, n, n % GT, XAL[:, :, P * n:P * (n + 1)], XAH[:, :, P * n:P * (n + 1)])
                    if g + 1 < G:
                        x_stats(g + 1)
                    dve.wait_ge(sp1["k_high"], g + 1)
                    nc.vector.tensor_tensor(K2[ROPE:P, GW * g:GW * (g + 1)], bank(1)[ROPE:P, :], b_kt[ROPE:P, :],
                                            ALU.subtract).then_inc(sp1["k_low"], 1)
                    for n in range(NEX):
                        dve.wait_ge(sp1["ex_high"], NEX * g + n + 1)
                        nc.vector.tensor_tensor(b_el[:, n % 2, :], bank(2 + n % 2), b_eh[:, n % 2, :],
                                                ALU.subtract).then_inc(sp1["ex_low"], 1)

            @block.scalar
            def _(act):
                act.wait_ge(sp1["w_loaded"], 16 * 4)
                nc.scalar.copy(b_wdh, b_wd.rearrange("p (c n) -> p c n", c=DC)).then_inc(sp1["wd_high"], 1)
                for g in range(G):
                    at = slice(GW * g, GW * (g + 1))
                    for t in range(GT):
                        n = GT * g + t
                        normalise(act, sb, n, g, t, b_x[:, g % 2, t, :], b_xn[:, t % 2, :], n >= 2)
                        high_half(act, sb, n, t, XAH[:, :, P * n:P * (n + 1)])
                    act.wait_ge(sp1["c_ps"], g + 1)
                    nc.scalar.copy(b_c, bank(0)).then_inc(sp1["c_sb"], 1)
                    act.wait_ge(sp1["k_ps"], g + 1)
                    if g > 0:
                        act.wait_ge(sp1["k_low"], g)
                    nc.scalar.copy(K2[0:ROPE, at], bank(1)[0:ROPE, :])
                    nc.scalar.copy(K1[0:ROPE, 0, at], bank(1)[0:ROPE, :])
                    nc.scalar.copy(K1[0:ROPE, 1, at], bank(1)[0:ROPE, :])
                    nc.scalar.copy(b_kt[ROPE:P, :], bank(1)[ROPE:P, :]).then_inc(sp1["k_high"], 1)
                    for n in range(NEX):
                        k = NEX * g + n
                        act.wait_ge(sp1["ex_ps"], NOUT * g + n + 1)
                        if k >= 2:
                            act.wait_ge(ex_stored[n % 2], 48 * (k // 2))
                        nc.scalar.copy(b_eh[:, n % 2, :], bank(2 + n % 2)).then_inc(sp1["ex_high"], 1)
                    for t in range(GT):
                        act.wait_ge(sp1["ex_ps"], NOUT * g + NEX + t + 1)
                        nc.scalar.copy(VA[:, GT * g + t, :], bank(2 + t % 2)).then_inc(sp1["v_copied"], 1)

            @block.tensor
            def _(pe):
                for g in range(G):
                    at = slice(GW * g, GW * (g + 1))
                    for t in range(GT):
                        n = GT * g + t
                        transpose(pe, sb, n, t, b_xn[:, t % 2, :], n - 3 if n >= 4 else None)
                    pe.wait_ge(sb["low"], GT * (g + 1))
                    pe.wait_ge(sp1["wd_low"], 1)
                    if g > 0:
                        pe.wait_ge(sp1["c_sb"], g)
                        pe.wait_ge(sp1["k_low"], g)
                    for k, signal in ((0, "c_ps"), (1, "k_ps")):
                        for c in range(DC):
                            last = split_products(nc, bank(k), b_wdh[:, c, P * k:P * (k + 1)],
                                                  b_wdl[:, c, P * k:P * (k + 1)], XAH[:, c, at], XAL[:, c, at],
                                                  c == 0, c == DC - 1)
                        last.then_inc(sp1[signal], 1)
                    pe.wait_ge(sp1["c_sb"], g + 1)
                    for n in range(NOUT):
                        if n >= 2 and n - 2 < NEX:
                            pe.wait_ge(sp1["ex_low"], NEX * g + n - 1)
                        elif n >= 2:
                            pe.wait_ge(sp1["v_copied"], GT * g + n - 2 - NEX + 1)
                        elif g > 0:
                            pe.wait_ge(sp1["v_copied"], GT * (g - 1) + GT - 1 + n)
                        c = n % DC
                        if n < DC:
                            w, r = WUP[0:ROPE, 0, P * c:P * (c + 1)], b_c[0:ROPE, :]
                        elif n < NEX:
                            w, r = WUP[ROPE:P, 0, P * c:P * (c + 1)], b_c[ROPE:P, :]
                        else:
                            w, r = b_c[ROPE:P, P * (n - NEX):P * (n - NEX + 1)], WUP[ROPE:P, 1, :]
                        nc.tensor.matmul(bank(2 + n % 2), w, r, start=True, stop=True).then_inc(sp1["ex_ps"], 1)

        m = dict((n, sem("m_" + n)) for n in (
            "ones", "vst_init", "wraw_loaded", "wr_high", "wr_low", "q_ps", "q_high1", "q_high", "q_low", "mx_ps", "maxed", "max_t",
            "neg_max", "waited", "scores", "exps", "vst", "pv", "pv_out"))
        ex_in = [sem(f"m_ex_in{n}") for n in range(G)]
        row_in = [sem(f"m_row_in{n}") for n in range(2)]
        sums_out = [sem(f"m_sums_out{n}") for n in range(G)]
        TURN = 8
        TURNS = UNITS // TURN
        ST = (psum[:, 0:1024], psum[:, 1024:2048])
        MX = (bank(4), bank(5))
        QR = bank(6)
        AUX = bank(7)
        PVO, TR = AUX[:, 0:S], AUX[0:8, S:S + P]

        def active(i, k, lag):
            return not isinstance(i, int) or 0 <= TURN * i + k - lag < UNITS

        def count(i, k, lag, per, off):
            return i * (TURN * per) + (per * (k - lag) + off)

        def wait_unit(eng, s, i, k, lag, per, off):
            if active(i, k, lag):
                eng.wait_ge(s, count(i, k, lag, per, off))

        def wait_dma(eng, sems, i, k, lag, per):
            n = len(sems)
            if active(i, k, lag):
                eng.wait_ge(sems[(k - lag) % n], i * (TURN // n * per) + ((k - lag) // n + 1) * per)

        def steps(eng, step):
            for k in range(TURN):
                step(eng, 0, k)
            with eng.Fori(1, TURNS - 1) as i:
                for k in range(TURN):
                    step(eng, i, k)
            for k in range(TURN):
                step(eng, TURNS - 1, k)
            for k in range(4):
                step(eng, TURNS, k)

        def more_pairs(i, k):
            return not (isinstance(i, int) and i == TURNS - 1 and k >= G)

        def sync_step(sp, i, k):
            tg, pair = k % G, i * 2 + k // G
            if active(i, k, 0):
                if tg == 0 and more_pairs(i, k):
                    sp.wait_ge(m["wr_low"], i * 2 + (k // G + 1))
                    sp.dma_start(WRAW[:, (k // G + 1) % 2, :], wrope[bass.ds(i * 2 + (k // G + 1), 1)].rearrange(
                        "a p n -> p (a n)")).then_inc(m["wraw_loaded"], 16)
                wait_unit(sp, m["scores"], i, k, 4, 2, 2)
                cols = slice(GW * tg, GW * (tg + 1))
                sp.dma_start(X1[ROPE:KROW, tg, :, :].bitcast(F32),
                             exq[bass.ds(pair * 2, 2), :, cols].rearrange("h r t -> r h t")
                             ).then_inc(ex_in[tg], 16)
                sp.dma_start(K1[ROPE:KROW, :, cols].bitcast(F32),
                             exk[bass.ds(pair * 2, 2), :, cols].rearrange("h r t -> r h t")
                             ).then_inc(ex_in[tg], 16)
            if active(i, k, 2):
                wait_unit(sp, m["neg_max"], i, k, 2, 1, 1)
                for h in range(2):
                    sp.dma_start(X1[KROW:KROW + 1, (k - 2) % G, h, :].bitcast(F32), NM[4 * h:4 * h + 4, k % 2, :].bitcast(F32)
                                 ).then_inc(row_in[k % 2], 16)
            if active(i, k, 4):
                wait_unit(sp, m["pv_out"], i, k, 4, 1, 1)
                p4, t4 = (i * 2 + (k - 4) // G), (k - 4) % G
                for j in range(4):
                    h, b = j // 2, j % 2
                    c0 = GW * t4 + S * b
                    sp.dma_start(att[:, bass.ds((p4 * 2 + h) * HD, HD), c0:c0 + S],
                                 OSB[32 * j:32 * j + 2 * HD, k % G, :]).then_inc(sums_out[k % G], 16)

        def pool_step(pool, i, k):
            tg = k % G
            if active(i, k, 0):
                pair = i * 2 + k // G
                wait_unit(pool, m["pv"], i, k, 4, 1, 1)
                nc.gpsimd.tensor_copy(VST[:, GT * tg:GT * (tg + 1), :, 0:HD],
                                      VA[:, GT * tg:GT * (tg + 1), bass.ds(pair * 8, 8)].rearrange(
                                          "p t (h d) -> p t h d", h=2)).then_inc(m["vst"], 1)
                if tg == 0 and more_pairs(i, k):
                    w = (k // G + 1) % 2
                    n = i * 2 + (k // G + 1)
                    split_rope(pool, i, k, w, n)

        def split_rope(pool, i, k, w, n):
            pool.wait_ge(m["wraw_loaded"], (n + 1) * 16)
            if not isinstance(i, int) or TURN * i + k > 0:
                pool.wait_ge(m["q_ps"], count(i, k, 0, 1, 0))
            pool.sem_inc(m["waited"], 1)
            nc.gpsimd.tensor_scalar(WRH[:, w, :], WRAW[:, w, :], 1.0, 1.0, ALU.mult,
                                    ALU.mult).then_inc(m["wr_high"], 1)
            pool.wait_ge(m["wr_high"], n + 1)
            nc.gpsimd.tensor_tensor(WRL[:, w, :], WRAW[:, w, :], WRH[:, w, :], ALU.subtract).then_inc(m["wr_low"], 1)

        def pe_step(pe, i, k):
            tg, w = k % G, k // G

            def maxima(j):
                h, b = j // 2, j % 2
                if j >= 2 or not (isinstance(i, int) and i * TURN + k - 1 == 0):
                    pe.wait_ge(m["maxed"], count(i, k, 1, 4, j - 1))
                t1 = (k - 1) % G
                for q in range(2):
                    last = nc.tensor.matmul(MX[j % 2][:, S * q:S * (q + 1)],
                                            X1[0:KM, t1, h, S * b + P * q:S * b + P * (q + 1)],
                                            K1[0:KM, h, GW * t1 + S * b:GW * t1 + S * (b + 1)], start=True, stop=True)
                last.then_inc(m["mx_ps"], 1)

            def queries(cs):
                for c in cs:
                    a = P * c
                    last = split_products(nc, QR, WRH[:, w, a:a + P], WRL[:, w, a:a + P],
                                          XAH[:, c, GW * tg:GW * (tg + 1)], XAL[:, c, GW * tg:GW * (tg + 1)], c == 0,
                                          c == DC - 1)
                return last

            if active(i, k, 2):
                wait_unit(pe, m["maxed"], i, k, 2, 4, 4)
                wait_unit(pe, m["pv_out"], i, k, 5, 1, 1)
                wait_unit(pe, m["neg_max"], i, k, 3, 1, 1)
                nc.tensor.transpose(TR, MXS[:, k % 2, :], ident[:, :]).then_inc(m["max_t"], 1)
            if active(i, k, 1):
                wait_unit(pe, m["q_high"], i, k, 1, 1, 1)
                wait_dma(pe, ex_in, i, k, 1, 32)
                maxima(0)
                maxima(1)
            if active(i, k, 0):
                if tg == 0:
                    pe.wait_ge(m["wr_low"], i * 2 + (w + 1))
                wait_unit(pe, m["q_low"], i, k, 1, 1, 1)
                queries((0, 1))
            if active(i, k, 1):
                maxima(2)
                maxima(3)
            if active(i, k, 0):
                queries((2, 3)).then_inc(m["q_ps"], 1)
            if active(i, k, 3):
                t3 = (k - 3) % G
                wait_dma(pe, row_in, i, k, 3, 32)
                wait_unit(pe, m["q_low"], i, k, 3, 1, 1)
                for h in range(2):
                    wait_unit(pe, m["exps"], i, k, 4, 2, h + 1)
                    for b in range(2):
                        for kt in range(2):
                            o = ST[h][:, 512 * b + S * kt:512 * b + S * (kt + 1)]
                            ks = slice(GW * t3 + S * b + P * kt, GW * t3 + S * b + P * (kt + 1))
                            qs = slice(S * b, S * (b + 1))
                            nc.tensor.matmul(o, K1[0:KROW + 1, h, ks], X1[0:KROW + 1, t3, h, qs], start=True,
                                             stop=False)
                            last = nc.tensor.matmul(o, K2[:, ks], X2[:, t3, h, qs], start=False, stop=True)
                    last.then_inc(m["scores"], 1)
            if active(i, k, 4):
                t4 = (k - 4) % G
                wait_unit(pe, m["exps"], i, k, 4, 2, 2)
                wait_unit(pe, m["vst"], i, k, 4, 1, 1)
                wait_unit(pe, m["neg_max"], i, k, 2, 1, 1)
                wait_unit(pe, m["pv_out"], i, k, 5, 1, 1)
                for kt in range(2):
                    for j in range(4):
                        h, b = j // 2, j % 2
                        last = nc.tensor.matmul(PVO[32 * j:32 * (j + 1), :], VST[:, GT * t4 + 2 * b + kt, h, :],
                                                PB[:, k % 2, 512 * j + S * kt:512 * j + S * (kt + 1)], start=(kt == 0),
                                                stop=(kt == 1))
                last.then_inc(m["pv"], 1)

        def act_step(act, i, k):
            tg = k % G
            if active(i, k, 2):
                wait_unit(act, m["max_t"], i, k, 2, 1, 1)
                wait_dma(act, row_in, i, k, 4, 32)
                nc.scalar.mul(NM[:, k % 2, :], TR, -1.0).then_inc(m["neg_max"], 1)
            if active(i, k, 0):
                wait_unit(act, m["q_ps"], i, k, 0, 1, 1)
                wait_unit(act, m["scores"], i, k, 4, 2, 2)
                nc.scalar.copy(X1[0:ROPE, tg, 0, :], QR[0:ROPE, :])
                nc.scalar.copy(X2[ROPE:P, tg, 0, :], QR[0:ROPE, :]).then_inc(m["q_high1"], 1)
                nc.scalar.copy(X1[0:ROPE, tg, 1, :], QR[ROPE:P, :])
                nc.scalar.copy(X2[ROPE:P, tg, 1, :], QR[ROPE:P, :]).then_inc(m["q_high"], 1)
            if active(i, k, 3):
                for h in range(2):
                    wait_unit(act, m["scores"], i, k, 3, 2, h + 1)
                    wait_unit(act, m["pv"], i, k, 5, 1, 1)
                    nc.scalar.activation(PB[:, (k - 3) % 2, 1024 * h:1024 * (h + 1)], ST[h], ACT.Exp,
                                         scale=SC).then_inc(m["exps"], 1)

        def dve_step(dve, i, k):
            tg = k % G
            if active(i, k, 1):
                wait_unit(dve, m["max_t"], i, k, 3, 1, 1)
                for j in range(4):
                    wait_unit(dve, m["mx_ps"], i, k, 1, 4, j + 1)
                    nc.vector.tensor_reduce(MXS[:, (k - 1) % 2, 2 * j:2 * j + 2],
                                            MX[j % 2].rearrange("p (q n) -> p q n", q=2), AXX,
                                            ALU.max).then_inc(m["maxed"], 1)
            if active(i, k, 0):
                wait_unit(dve, m["q_high1"], i, k, 0, 1, 1)
                nc.vector.tensor_tensor(X2[0:ROPE, tg, 0, :], QR[0:ROPE, :], X1[0:ROPE, tg, 0, :], ALU.subtract)
                wait_unit(dve, m["q_high"], i, k, 0, 1, 1)
                nc.vector.tensor_tensor(X2[0:ROPE, tg, 1, :], QR[ROPE:P, :], X2[ROPE:P, tg, 1, :],
                                        ALU.subtract).then_inc(m["q_low"], 1)
            if active(i, k, 4):
                wait_unit(dve, m["pv"], i, k, 4, 1, 1)
                wait_dma(dve, sums_out, i, k, 8, 64)
                nc.vector.tensor_copy(OSB[:, k % G, :], PVO).then_inc(m["pv_out"], 1)

        with nc.Block() as block:
            @block.sync
            def _(sp):
                sp.dma_start(WRAW[:, 0, :], wrope[0]).then_inc(m["wraw_loaded"], 16)
                sp.wait_ge(m["ones"], 1)
                steps(sp, sync_step)
                for n in range(G):
                    sp.wait_ge(sums_out[n], 64 * UNITS // G)

            @block.gpsimd
            def _(pool):
                nc.gpsimd.memset(VST[:, :, :, :], 0.0).then_inc(m["vst_init"], 1)
                pool.wait_ge(m["vst_init"], 1)
                nc.gpsimd.memset(VST[:, :, :, HD:2 * HD], 1.0).then_inc(m["vst_init"], 1)
                pool.wait_ge(m["vst_init"], 2)
                split_rope(pool, 0, 0, 0, 0)
                steps(pool, pool_step)

            @block.vector
            def _(dve):
                nc.vector.memset(K1[ROPE:96, :, :].bitcast(F32), 1.0).then_inc(m["ones"], 1)
                steps(dve, dve_step)

            @block.scalar
            def _(act):
                steps(act, act_step)

            @block.tensor
            def _(pe):
                steps(pe, pe_step)

        sc = dense_sems("c_")
        NWO = 2
        num = (XN[:, 0, :], SG[:, :])
        den = (XN[:, 1, :], HF[:, :])
        o = dict((n, sem("o_" + n)) for n in ("recip", "quotient"))
        sums_in = [sem(f"o_sums_in{n}") for n in range(2)]

        def ot(W, Z, g):
            return Z[:, :, :] if g % 2 == 0 else half(W, 1).rearrange("p (c n) -> p c n", c=DC)

        with nc.Block() as block:
            @block.sync
            def _(sp):
                for n in range(NWO):
                    if n > 0:
                        sp.wait_ge(sc["raw_read"], n)
                    sp.dma_start(RAW[:, 0:DC * D // NWO], wo[:, DC * D // NWO * n:DC * D // NWO * (n + 1)]
                                 ).then_inc(sc["raw_loaded"], 16)
                load_chunks(sp, sc, NWO)
                for g in range(G):
                    sp.wait_ge(sc["residual"], NT + GT * (g + 1))
                    sp.dma_start(out[GT * g:GT * (g + 1)].rearrange("t p d -> p t d"),
                                 X[:, GT * g:GT * (g + 1), :]).then_inc(sc["stored"], 16)
                sp.wait_ge(sc["stored"], 16 * G)

            @block.gpsimd
            def _(pool):
                for n in range(NWO):
                    split_piece(pool, sc, n, L0_AT + n * (DC * D // NWO), DC * D // NWO, False)
                for i in range(NI):
                    if i == 6:
                        inverse_root(pool, sc, 0)
                    if i * CW == L0_AT:
                        pool.wait_ge(sc["products"], NT)
                    split_piece(pool, sc, NWO + i, i * CW, CW, True)
                for n in range(1, G):
                    inverse_root(pool, sc, n)

            @block.tensor
            def _(pe):
                pe.wait_ge(sc["raw_read"], NWO)
                for g in range(G):
                    pe.wait_ge(sc["low"], DC * (g + 1))
                    for t in range(GT):
                        if g > 0:
                            pe.wait_ge(sc["residual"], GT * (g - 1) + t + 1)
                        for c in range(DC):
                            wh, wl = (half(W, 0)[:, D * c:D * (c + 1)] for W in (WH, WL))
                            last = split_products(nc, bank(t), ot(WH, XTH, g)[:, c, P * t:P * (t + 1)],
                                                  ot(WL, XTL, g)[:, c, P * t:P * (t + 1)], wh, wl, c == 0,
                                                  c == DC - 1)
                        last.then_inc(sc["products"], 1)
                for t in range(GT):
                    transpose(pe, sc, t, t, XN[:, t % 2, :], None)
                with pe.Fori(0, G - 1) as g:
                    ffn_pe(pe, sc, g * GT + NT, g, g * GT + GT, True)
                ffn_pe(pe, sc, 2 * NT - GT, G - 1, 0, False)

            @block.scalar
            def _(act):
                for g in range(G):
                    act.dma_start(X[:, GT * g:GT * (g + 1), :], x_mid[GT * g:GT * (g + 1)].rearrange("t p d -> p t d")
                                  ).then_inc(sc["loaded"], 16)
                for n in range(G * DC + 1):
                    if n < G * DC:
                        g, c = n // DC, n % DC
                        if n >= 2:
                            act.wait_ge(sc["low"], n - 1)
                        for k, dst in ((0, num[n % 2]), (1, den[n % 2])):
                            act.dma_start(dst, att[k, P * c:P * (c + 1), GW * g:GW * (g + 1)]
                                          ).then_inc(sums_in[n % 2], 16)
                    if n >= 1:
                        g, c = (n - 1) // DC, (n - 1) % DC
                        act.wait_ge(o["quotient"], n)
                        if g >= 2:
                            act.wait_ge(sc["products"], GT * (g - 1))
                        nc.scalar.copy(ot(WH, XTH, g)[:, c, :], num[(n - 1) % 2]).then_inc(sc["high"], 1)
                for t in range(GT):
                    normalise(act, sc, t, 0, t, X[:, t, :], XN[:, t % 2, :], t >= 2)
                    high_half(act, sc, t, t, xt(XTH, t))
                with act.Fori(0, G - 1) as g:
                    ffn_act(act, sc, g * GT + NT, g, g * GT + GT, g + 1, g * GT + GT, True)
                ffn_act(act, sc, 2 * NT - GT, G - 1, 0, 0, 0, False)

            @block.vector
            def _(dve):
                def add_projection(g):
                    for t in range(GT):
                        dve.wait_ge(sc["products"], GT * g + t + 1)
                        residual(sc, t, GT * g, 1.0, sc["residual"])

                for n in range(G * DC):
                    g, c = n // DC, n % DC
                    dve.wait_ge(sums_in[n % 2], 32 * (n // 2 + 1))
                    nc.vector.reciprocal(den[n % 2], den[n % 2]).then_inc(o["recip"], 1)
                    dve.wait_ge(o["recip"], n + 1)
                    nc.vector.tensor_tensor(num[n % 2], num[n % 2], den[n % 2], ALU.mult).then_inc(o["quotient"], 1)
                    dve.wait_ge(sc["high"], n + 1)
                    nc.vector.tensor_tensor(ot(WL, XTL, g)[:, c, :], num[n % 2], ot(WH, XTH, g)[:, c, :],
                                            ALU.subtract).then_inc(sc["low"], 1)
                    if n == DC:
                        dve.wait_ge(sc["loaded"], 16 * G)
                    if c == 0 and g > 0:
                        add_projection(g - 1)
                add_projection(G - 1)
                dve.wait_ge(sc["residual"], GT)
                group_stats(dve, sc, 0, [X[:, t, :] for t in range(GT)])
                for t in range(GT):
                    low_half(dve, sc, NT + t, t, xt(XTL, t), xt(XTH, t))
                with dve.Fori(0, G - 1) as g:
                    ffn_dve(dve, sc, g * GT + NT, g, g * GT + GT, g + 1, g * GT, g * GT + GT, True, g * GT + 2 * GT)
                ffn_dve(dve, sc, 2 * NT - GT, G - 1, 0, 0, NT - GT, 0, False, 0)


_ORDER = ("x", "wT", "mwT", "maskT", "a_er", "b_er", "coef", "scal", "bias", "ffw", "wdown", "wqu", "wku", "wvu",
          "wrope", "wo")


def kernel(**inputs):
    import numpy as np
    import concourse.bacc as bacc
    from concourse.bass_utils import run_bass_kernel_spmd

    a = {k: np.asarray(v) for k, v in inputs.items()}
    data = a["L0_attn_data"]

    def rows(w):
        return np.ascontiguousarray(w.reshape(DC, P, -1).transpose(1, 0, 2).reshape(P, -1))

    gu, dn = a["L1_ffn_w_gate_up"], a["L1_ffn_w_down"]
    ffw = np.zeros((NI, P, CW), gu.dtype)
    for i in range(NI):
        n = min(P, I_FF - P * i)
        for k in range(2):
            w = gu[k * I_FF + P * i:k * I_FF + P * i + n].T.reshape(DC, P, n).transpose(1, 0, 2)
            ffw[i, :, k * D:(k + 1) * D].reshape(P, DC, P)[:, :, :n] = w
        ffw[i, :n, 2 * D:] = dn[:, P * i:P * i + n].T
    krope = a["L1_attn_Wk_rope"]
    wr = a["L1_attn_Wq_rope"].reshape(DC, P, NHP, P).transpose(2, 1, 0, 3).reshape(NHP, P, DC * P)
    laid = {
        "x": data.reshape(NT, P, D),
        "wT": rows(a["L0_ffn_W"].T),
        "mwT": rows(a["L0_attn_weight"].T),
        "maskT": rows(a["L0_attn_mask"].T),
        "a_er": a["L0_ffn_A"].reshape(2, P, D).transpose(1, 0, 2),
        "b_er": a["L0_ffn_Bf"].transpose(0, 2, 1).reshape(2, P, D).transpose(1, 0, 2),
        "coef": np.repeat(a["L0_ffn_coeffs"], 16).reshape(2, P).T,
        "scal": np.repeat(a["L0_ffn_scales"], 16).reshape(2, P).T,
        "bias": a["L0_ffn_bias"].reshape(1, D),
        "ffw": ffw,
        "wdown": rows(np.concatenate([a["L1_attn_Wq_down"], a["L1_attn_Wkv_down"], krope, krope], axis=1)),
        "wqu": a["L1_attn_Wq_up"],
        "wku": a["L1_attn_Wk_up"],
        "wvu": a["L1_attn_Wv_up"],
        "wrope": wr,
        "wo": rows(a["L1_attn_Wo"]),
    }
    nc = bacc.Bacc("TRN2", target_bir_lowering=False, num_devices=1)
    arrays, args = {}, []
    for name in _ORDER:
        v = np.ascontiguousarray(laid[name])
        arrays["in_" + name] = v
        args.append(nc.dram_tensor("in_" + name, v.shape, mybir.dt.from_np(v.dtype), kind="ExternalInput").ap())
    out = nc.dram_tensor("out", (NT, P, D), F32, kind="ExternalOutput").ap()
    build(nc, *args, out)
    got = run_bass_kernel_spmd(nc, [arrays], core_ids=[0]).results[0]["out"]
    return got.reshape(data.shape)
```

```python
import concourse.bass as bass
from concourse import mybir
from contextlib import ExitStack

F32 = mybir.dt.float32
F32R = mybir.dt.float32r
I32 = mybir.dt.int32
ALU = mybir.AluOpType
ACT = mybir.ActivationFunctionType
AXX = mybir.AxisListType.X

P = 128
TOK, D = 2048, 512
NT = TOK // P
G = 4
GT = NT // G
GW = GT * P
DC = D // P
S = 256
ER = 256
MB = 32
I_FF = 1376
NI = -(-I_FF // P)
PW = 3 * D // 2
CW = 3 * D
L0_AT = 8 * CW
H = 128
HD, ROPE = 4, 64
NHP = H // 2
UNITS = NHP * G
SC = float(HD + ROPE) ** -0.5
EX = 3 * HD
KM = ROPE + HD
KROW = ROPE + EX
EPS = 1e-5


def split_products(nc, out, hi_w, lo_w, hi_x, lo_x, first, last):
    nc.tensor.matmul(out, hi_w, hi_x, start=first, stop=False)
    nc.tensor.matmul(out, lo_w, hi_x, start=False, stop=False)
    return nc.tensor.matmul(out, hi_w, lo_x, start=False, stop=last)


def build(nc, x, wT, mwT, maskT, a_er, b_er, coef, scal, bias, ffw, wdown, wqu, wku, wvu, wrope, wo, out):
    ctx = ExitStack()
    with ctx:
        def sem(name):
            return ctx.enter_context(nc.semaphore(name))

        def sbuf(stack, name, shape, dt):
            return stack.enter_context(nc.sbuf_tensor(name, shape, dt))

        x_mid = nc.dram_tensor("x_mid", (NT, P, D), F32).ap()
        exq = nc.dram_tensor("exq", (H, EX, TOK), F32).ap()
        exk = nc.dram_tensor("exk", (H, EX, TOK), F32).ap()
        att = nc.dram_tensor("att", (H, HD + 1, TOK), F32).ap()

        psum = ctx.enter_context(nc.psum_tensor("psum", [P, 8 * 512], F32))

        def bank(n):
            return psum[:, 512 * n:512 * n + 512]

        ident = sbuf(ctx, "ident", [P, P], F32)
        stat = sbuf(ctx, "stat", [P, GT, 6], F32)
        mv = sbuf(ctx, "mv", [P, GT, 2], F32)
        rstd = sbuf(ctx, "rstd", [P, GT], F32)
        nbias = sbuf(ctx, "nbias", [P, GT], F32)
        veps = sbuf(ctx, "veps", [P, GT], F32)
        minus_half = sbuf(ctx, "minus_half", [P, GT], F32)

        set_a = ExitStack()
        X = sbuf(set_a, "X", [P, NT, D], F32)
        WH = sbuf(set_a, "WH", [P, NI * CW], F32R)
        WL = sbuf(set_a, "WL", [P, NI * CW], F32R)
        bias_half = sbuf(set_a, "bias_half", [P, D], F32)
        setup = ExitStack()
        s_wT = sbuf(setup, "s_wT", [P, DC * D], F32)
        s_mw = sbuf(setup, "s_mw", [P, DC * D], F32)
        s_mask = sbuf(setup, "s_mask", [P, DC * D], I32)
        s_a = sbuf(setup, "s_a", [P, 2, D], F32)
        s_b = sbuf(setup, "s_b", [P, 2, D], F32)
        s_coef = sbuf(setup, "s_coef", [P, 2], F32)
        s_scal = sbuf(setup, "s_scal", [P, 2], F32)
        s_bias = sbuf(setup, "s_bias", [1, D], F32)
        s_ones = sbuf(setup, "s_ones", [1, P], F32)
        s_bd = sbuf(setup, "s_bd", [P, P], F32)
        s_cnt = sbuf(setup, "s_cnt", [P, DC * D // MB], F32)
        s_keep = sbuf(setup, "s_keep", [P, DC * D // MB], F32)
        setup.close()
        XTH = sbuf(set_a, "XTH", [P, DC, GW], F32R)
        XTL = sbuf(set_a, "XTL", [P, DC, GW], F32R)
        HH = sbuf(set_a, "HH", [P, 2, GW], F32R)
        HL = sbuf(set_a, "HL", [P, 2, GW], F32R)
        XN = sbuf(set_a, "XN", [P, 2, D], F32)
        RAW = sbuf(set_a, "RAW", [P, 2, CW // 2], F32)
        spread = sbuf(set_a, "spread", [P, DC, P], F32)
        SG = sbuf(set_a, "SG", [P, GW], F32)
        HF = sbuf(set_a, "HF", [P, GW], F32)
        set_a.close()

        set_b = ExitStack()
        XAH = sbuf(set_b, "XAH", [P, DC, TOK], F32R)
        XAL = sbuf(set_b, "XAL", [P, DC, TOK], F32R)
        K1 = sbuf(set_b, "K1", [P, 2, TOK], F32R)
        K2 = sbuf(set_b, "K2", [P, TOK], F32R)
        X1 = sbuf(set_b, "X1", [P, G, 2, GW], F32R)
        X2 = sbuf(set_b, "X2", [P, G, 2, GW], F32R)
        WRH = sbuf(set_b, "WRH", [P, 2, DC * P], F32R)
        WRL = sbuf(set_b, "WRL", [P, 2, DC * P], F32R)
        NM = sbuf(set_b, "NM", [8, 2, P], F32R)
        PB = sbuf(set_b, "PB", [P, 2, 4 * 512], F32)
        WRAW = sbuf(set_b, "WRAW", [P, 2, DC * P], F32)
        VST = sbuf(set_b, "VST", [P, NT, 2, 32], F32)
        VA = sbuf(set_b, "VA", [P, NT, D], F32)
        OSB = sbuf(set_b, "OSB", [P, G, S], F32)
        WUP = sbuf(set_b, "WUP", [P, 2, D], F32)
        MXS = sbuf(set_b, "MXS", [P, 2, 8], F32)
        b_xn = sbuf(set_b, "b_xn", [P, 2, D], F32)
        b_wdh = sbuf(set_b, "b_wdh", [P, DC, 2 * P], F32R)
        b_wdl = sbuf(set_b, "b_wdl", [P, DC, 2 * P], F32R)
        b_x = PB[:, :, :].rearrange("p a (t d) -> p a t d", t=GT)
        b_wd = VST[:, :, :, :].rearrange("p a b c -> p (a b c)")
        b_kt = X2[:, 0, 0, :]
        b_up = (WUP[:, 0, :], WUP[:, 1, :], OSB[:, 0:2, :].rearrange("p a b -> p (a b)"))
        b_uph = tuple(X2[:, n // 2, n % 2, :] for n in (1, 2, 3))
        b_upl = tuple(X2[:, n // 2, n % 2, :] for n in (4, 5, 6))
        b_cq, b_ckv = WRH[:, 1, :], WRL[:, 1, :]
        b_eh = X1[:, 0:2, :, :].rearrange("p a b n -> p (a b) n")
        b_el = X1[:, 2:4, :, :].rearrange("p a b n -> p (a b) n")
        set_b.close()

        x_loaded = [sem(f"x_loaded{g}") for g in range(G)]
        loaded = dict((n, sem("loaded_" + n)) for n in ("updates", "bias", "mask", "wT", "mw"))
        setup_done = sem("setup_done")
        wts = dict((n, sem(n)) for n in ("w_ready", "b_ready", "cnt_ready", "cnt_sum", "keep_ready", "upd_done",
                                         "weff_done", "mw_done", "wh_done", "bias_bc", "ident0", "ident_done",
                                         "consts_done"))

        def half(W, n):
            return W[:, L0_AT + n * DC * D:L0_AT + (n + 1) * DC * D]

        with nc.Block() as block:
            @block.sync
            def _(sp):
                for dst, src, signal in ((s_coef[:, :], coef, "updates"), (s_scal[:, :], scal, "updates"),
                                         (s_b[:, :, :], b_er, "updates"), (s_a[:, :, :], a_er, "updates"),
                                         (s_bias[:, :], bias, "bias"), (s_mask[:, :], maskT, "mask"),
                                         (s_wT[:, :], wT, "wT"), (s_mw[:, :], mwT, "mw")):
                    sp.dma_start(dst, src).then_inc(loaded[signal], 16)
                for g in range(G):
                    sp.dma_start(X[:, GT * g:GT * (g + 1), :],
                                 x[GT * g:GT * (g + 1)].rearrange("t p d -> p t d")).then_inc(x_loaded[g], 16)

            @block.gpsimd
            def _(pool):
                nc.gpsimd.memset(ident[:, :], 0.0).then_inc(wts["ident0"], 1)
                pool.wait_ge(wts["ident0"], 1)
                nc.gpsimd.affine_select(out=ident[:, :], in_=ident[:, :], compare_op=ALU.not_equal, fill=1.0, base=0,
                                        pattern=[[-1, P]], channel_multiplier=1).then_inc(wts["ident_done"], 1)

            @block.vector
            def _(dve):
                nc.vector.memset(s_bd[:, :], 0.0).then_inc(wts["consts_done"], 1)
                nc.vector.memset(s_ones[:, :], 1.0).then_inc(wts["consts_done"], 1)
                dve.wait_ge(wts["consts_done"], 2)
                for n in range(P // MB):
                    nc.vector.memset(s_bd[MB * n:MB * (n + 1), MB * n:MB * (n + 1)], 1.0).then_inc(wts["consts_done"], 1)
                dve.wait_ge(loaded["updates"], 4 * 16)
                nc.vector.tensor_tensor(s_coef[:, :], s_coef[:, :], s_scal[:, :], ALU.mult).then_inc(wts["w_ready"], 1)
                dve.wait_ge(wts["w_ready"], 1)
                for k in range(2):
                    nc.vector.tensor_scalar(s_b[:, k, :], s_b[:, k, :], s_coef[:, k:k + 1], None,
                                            ALU.mult).then_inc(wts["b_ready"], 1)
                dve.wait_ge(loaded["mask"], 16)
                nc.vector.tensor_reduce(s_cnt[:, :], s_mask[:, :].rearrange("p (n m) -> p n m", m=MB), AXX,
                                        ALU.add).then_inc(wts["cnt_ready"], 1)
                dve.wait_ge(wts["bias_bc"], 1)
                nc.vector.tensor_scalar(bias_half[:, :], bank(5), 0.5, None, ALU.mult).then_inc(setup_done, 1)
                dve.wait_ge(wts["cnt_sum"], 1)
                nc.vector.tensor_scalar(s_keep[:, :], bank(4)[:, 0:DC * D // MB], 0.0, None,
                                        ALU.is_gt).then_inc(wts["keep_ready"], 1)
                dve.wait_ge(loaded["wT"], 16)
                for c in range(DC):
                    dve.wait_ge(wts["upd_done"], c + 1)
                    nc.vector.tensor_tensor(s_wT[:, D * c:D * (c + 1)], bank(c), s_wT[:, D * c:D * (c + 1)],
                                            ALU.add).then_inc(wts["weff_done"], 1)
                dve.wait_ge(wts["keep_ready"], 1)
                dve.wait_ge(loaded["mw"], 16)
                m3 = s_mw[:, :].rearrange("p (n m) -> p n m", m=MB)
                nc.vector.tensor_tensor(m3, m3, s_keep[:, :].unsqueeze(2).broadcast_to([P, DC * D // MB, MB]),
                                        ALU.mult).then_inc(wts["mw_done"], 1)
                dve.wait_ge(wts["wh_done"], 1)
                nc.vector.tensor_tensor(half(WL, 0), s_wT[:, :], half(WH, 0), ALU.subtract).then_inc(setup_done, 1)
                dve.wait_ge(wts["wh_done"], 2)
                nc.vector.tensor_tensor(half(WL, 1), s_mw[:, :], half(WH, 1), ALU.subtract).then_inc(setup_done, 1)

            @block.scalar
            def _(act):
                act.wait_ge(wts["weff_done"], DC)
                nc.scalar.copy(half(WH, 0), s_wT[:, :]).then_inc(wts["wh_done"], 1)
                act.wait_ge(wts["mw_done"], 1)
                nc.scalar.copy(half(WH, 1), s_mw[:, :]).then_inc(wts["wh_done"], 1)

            @block.tensor
            def _(pe):
                pe.wait_ge(loaded["bias"], 16)
                pe.wait_ge(wts["consts_done"], 2 + P // MB)
                pe.wait_ge(wts["b_ready"], 2)
                for c in range(DC):
                    for k in range(2):
                        last = nc.tensor.matmul(bank(c), s_a[:, k, P * c:P * (c + 1)], s_b[:, k, :], start=(k == 0),
                                                stop=(k == 1))
                    last.then_inc(wts["upd_done"], 1)
                nc.tensor.matmul(bank(5), s_ones[:, :], s_bias[:, :], start=True, stop=True).then_inc(wts["bias_bc"], 1)
                pe.wait_ge(wts["cnt_ready"], 1)
                nc.tensor.matmul(bank(4)[:, 0:DC * D // MB], s_bd[:, :], s_cnt[:, :], start=True,
                                 stop=True).then_inc(wts["cnt_sum"], 1)

        NORM = ("stat_step", "waited", "var", "rstd", "stats", "normed", "transposed", "high", "low")
        FFN = ("raw_high", "raw_read", "split", "products", "residual", "gate_up", "gated", "hidden", "hidden_high",
               "hidden_low", "down", "stored")

        def dense_sems(tag, names):
            return dict((n, sem(tag + n)) for n in names)

        def tp_bank(t):
            return bank(4 + (t + 2) % 4)

        def moments(dve, s, n, srcs):
            for t in range(GT):
                nc.vector.bn_stats(stat[:, t, :], srcs[t]).then_inc(s["stat_step"], 1)
            dve.wait_ge(s["stat_step"], n * (2 * GT) + GT)
            dve.sem_inc(s["waited"], 1)
            for t in range(GT):
                nc.vector.bn_aggr(mv[:, t, :], stat[:, t, :]).then_inc(s["stat_step"], 1)
            dve.wait_ge(s["stat_step"], n * (2 * GT) + 2 * GT)
            nc.vector.tensor_scalar(veps[:, :], mv[:, :, 1], EPS, None, ALU.add).then_inc(s["var"], 1)

        def offsets(dve, s, n):
            dve.wait_ge(s["rstd"], n + 1)
            nc.vector.scalar_tensor_tensor(out=nbias[:, :], in0=mv[:, :, 0], scalar=-1.0, in1=rstd[:, :],
                                           op0=ALU.mult, op1=ALU.mult).then_inc(s["stats"], 1)

        def inverse_root(pool, s, n):
            pool.wait_ge(s["var"], n + 1)
            if n > 0:
                pool.wait_ge(s["normed"], GT * n)
            nc.gpsimd.tensor_tensor(rstd[:, :], veps[:, :], minus_half[:, :], ALU.pow).then_inc(s["rstd"], 1)

        def normalise(act, s, n, group, t, src, dst, wait_slot):
            act.wait_ge(s["stats"], group + 1)
            if wait_slot:
                act.wait_ge(s["transposed"], n - 1)
            nc.scalar.activation(dst, src, ACT.Identity, bias=nbias[:, t:t + 1],
                                 scale=rstd[:, t:t + 1]).then_inc(s["normed"], 1)

        def transpose(pe, s, n, t, src, wait_bank):
            pe.wait_ge(s["normed"], n + 1)
            if wait_bank is not None:
                pe.wait_ge(s["low"], wait_bank)
            for c in range(DC):
                last = nc.tensor.transpose(tp_bank(t)[:, P * c:P * (c + 1)], src[:, P * c:P * (c + 1)], ident[:, :])
            last.then_inc(s["transposed"], 1)

        def chunks(ap):
            return ap.rearrange("p (c n) -> p c n", c=DC)

        def high_half(act, s, n, t, dst):
            act.wait_ge(s["transposed"], n + 1)
            nc.scalar.copy(dst, chunks(tp_bank(t))).then_inc(s["high"], 1)

        def low_half(dve, s, m, t, dst, high):
            dve.wait_ge(s["high"], m + 1)
            nc.vector.tensor_tensor(dst, chunks(tp_bank(t)), high, ALU.subtract).then_inc(s["low"], 1)

        def xt(W, t):
            return W[:, :, P * t:P * (t + 1)]

        def xtile(T):
            return X[:, bass.ds(T, 1), :].rearrange("p a d -> p (a d)")

        def linear_pe(pe, s, m, w):
            def product(t):
                pe.wait_ge(s["low"], m + (t + 1))
                if not isinstance(m, int) or m + t >= 4:
                    pe.wait_ge(s["residual"], m + (t - 3))
                for c in range(DC):
                    wh, wl = (half(W, w)[:, D * c:D * (c + 1)] for W in (WH, WL))
                    last = split_products(nc, bank(t), XTH[:, c, P * t:P * (t + 1)], XTL[:, c, P * t:P * (t + 1)], wh,
                                          wl, c == 0, c == DC - 1)
                last.then_inc(s["products"], 1)

            product(0)
            for t in range(GT):
                if t + 1 < GT:
                    product(t + 1)
                transpose(pe, s, m + (t + 4), t, XN[:, t % 2, :], m + (t + 1))

        def linear_act(act, s, m, n, T_next):
            for t in range(GT):
                normalise(act, s, m + (t + 4), n + 1, t, xtile(T_next + t), XN[:, t % 2, :], True)
                if t > 0:
                    high_half(act, s, m + (t + 3), t - 1, xt(XTH, t - 1))
            high_half(act, s, m + (GT + 3), GT - 1, xt(XTH, GT - 1))

        def linear_dve(dve, s, m, n, T, T_later, bias_at):
            dve.wait_ge(s["normed"], m + GT)
            offsets(dve, s, n + 1)
            for t in range(GT):
                dve.wait_ge(s["products"], m + (t + 1))
                if bias_at is None:
                    residual(s, t, T, 1.0, s["residual"])
                else:
                    residual(s, t, T, 0.5, s["acc"])
                    dve.wait_ge(s["acc"], bias_at + (t + 1))
                    nc.vector.tensor_tensor(xtile(T + t), xtile(T + t), bias_half[:, :],
                                            ALU.add).then_inc(s["residual"], 1)
                if t == 2 and T_later is not None:
                    dve.wait_ge(s["residual"], m + 1)
                    moments(dve, s, n + 2, [xtile(T_later + u) for u in range(GT)])
                if t > 0:
                    low_half(dve, s, m + (t + 3), t - 1, xt(XTL, t - 1), xt(XTH, t - 1))
            low_half(dve, s, m + (GT + 3), GT - 1, xt(XTL, GT - 1), xt(XTH, GT - 1))

        def residual(s, t, T, factor, signal):
            nc.vector.scalar_tensor_tensor(out=xtile(T + t), in0=bank(t), scalar=factor, in1=xtile(T + t),
                                           op0=ALU.mult, op1=ALU.add).then_inc(signal, 1)

        def gate_up(pe, s, m, g, i):
            if i == 0:
                pe.wait_ge(s["low"], m + GT)
            elif i >= 2:
                pe.wait_ge(s["hidden"], g * NI + (i - 1))
            pe.wait_ge(s["split"], i + 1)
            for k in range(2):
                for c in range(DC):
                    a = i * CW + k * D + c * P
                    last = split_products(nc, bank(4 + 2 * (i % 2) + k), WH[:, a:a + P], WL[:, a:a + P], XTH[:, c, :],
                                          XTL[:, c, :], c == 0, c == DC - 1)
            last.then_inc(s["gate_up"], 1)

        def down(pe, s, m, g, i, wait_banks):
            pe.wait_ge(s["hidden_low"], g * NI + (i + 1))
            if i == 0 and wait_banks:
                pe.wait_ge(s["residual"], m)
            a = i * CW + 2 * D
            for t in range(GT):
                hh, hl = (W[:, i % 2, P * t:P * (t + 1)] for W in (HH, HL))
                last = split_products(nc, bank(t), hh, hl, WH[:, a:a + D], WL[:, a:a + D], i == 0, i == NI - 1)
                if i == NI - 1:
                    last.then_inc(s["products"], 1)
            if i < NI - 1:
                last.then_inc(s["down"], 1)

        def ffn_pe(pe, s, m, g, ln, ahead):
            for i in range(NI):
                gate_up(pe, s, m, g, i)
                if i > 0:
                    down(pe, s, m, g, i - 1, True)
            if ahead:
                for t in (0, 1):
                    transpose(pe, s, ln + t, t, XN[:, t % 2, :], None)
            down(pe, s, m, g, NI - 1, True)
            if ahead:
                for t in (2, 3):
                    transpose(pe, s, ln + t, t, XN[:, t % 2, :], None)

        def ffn_act(act, s, m, g, ln, n, T_next, ahead):
            for i in range(NI):
                b = bank(4 + 2 * (i % 2))
                act.wait_ge(s["gate_up"], g * NI + (i + 1))
                if i > 0:
                    act.wait_ge(s["hidden"], g * NI + i)
                nc.scalar.activation(SG[:, :], b, ACT.Silu).then_inc(s["gated"], 1)
                act.wait_ge(s["hidden"], g * NI + (i + 1))
                if i >= 2:
                    act.wait_ge(s["down"], g * (NI - 1) + (i - 1))
                nc.scalar.copy(HH[:, i % 2, :], HF[:, :]).then_inc(s["hidden_high"], 1)
                if ahead and i == 8:
                    for t in (0, 1):
                        normalise(act, s, ln + t, n, t, xtile(T_next + t), XN[:, t % 2, :], True)
            if ahead:
                for t in range(GT):
                    high_half(act, s, ln + t, t, xt(XTH, t))
                    if t < 2:
                        normalise(act, s, ln + (t + 2), n, t + 2, xtile(T_next + (t + 2)), XN[:, t % 2, :], True)

        def ffn_dve(dve, s, m, g, ln, n, T, T_next, ahead, prior):
            for i in range(NI):
                dve.wait_ge(s["gated"], g * NI + (i + 1))
                if i > 0:
                    dve.wait_ge(s["hidden_low"], g * NI + i)
                nc.vector.tensor_tensor(HF[:, :], bank(5 + 2 * (i % 2)), SG[:, :], ALU.mult).then_inc(s["hidden"], 1)
                if ahead and i == 4:
                    dve.wait_ge(s["residual"], prior)
                    moments(dve, s, n, [xtile(T_next + t) for t in range(GT)])
                if ahead and i == 5:
                    dve.wait_ge(s["normed"], ln)
                    offsets(dve, s, n)
                dve.wait_ge(s["hidden_high"], g * NI + (i + 1))
                if i >= 2:
                    dve.wait_ge(s["down"], g * (NI - 1) + (i - 1))
                nc.vector.tensor_tensor(HL[:, i % 2, :], HF[:, :], HH[:, i % 2, :],
                                        ALU.subtract).then_inc(s["hidden_low"], 1)
            order = [("low", 0), ("low", 1), ("res", 0), ("res", 1), ("res", 2), ("low", 2), ("low", 3), ("res", 3)]
            for what, t in order:
                if what == "low" and ahead:
                    low_half(dve, s, m + (t + 4), t, xt(XTL, t), xt(XTH, t))
                elif what == "res":
                    dve.wait_ge(s["products"], m + (t + 1))
                    residual(s, t, T, 0.5, s["residual"])

        def pieces(i):
            return [(ffw[i][:, PW * k:PW * (k + 1)], i * CW + PW * k, PW, i if k else None) for k in range(2)]

        def load_pieces(sp, s, todo, raw_in):
            for n, (src, _, width, _) in enumerate(todo):
                if n >= 2:
                    sp.wait_ge(s["raw_read"], n - 1)
                sp.dma_start(RAW[:, n % 2, 0:width], src).then_inc(raw_in[n % 2], 16)

        def split_piece(pool, s, raw_in, n, piece):
            _, a, width, chunk = piece
            raw = RAW[:, n % 2, 0:width]
            pool.wait_ge(raw_in[n % 2], 16 * (n // 2 + 1))
            nc.gpsimd.tensor_scalar(WH[:, a:a + width], raw, 1.0, 1.0, ALU.mult, ALU.mult).then_inc(s["raw_high"], 1)
            pool.wait_ge(s["raw_high"], n + 1)
            nc.gpsimd.tensor_tensor(WL[:, a:a + width], raw, WH[:, a:a + width], ALU.subtract).then_inc(s["raw_read"], 1)
            if chunk is not None:
                pool.wait_ge(s["raw_read"], n + 1)
                pool.sem_inc(s["split"], 1)

        sa = dense_sems("a_", NORM + FFN + ("acc", "consts"))
        raw_in = [sem(f"a_raw_in{n}") for n in range(2)]
        todo = [p for i in range(NI) for p in pieces(i)]
        LAYERS = (0, 1, 0)
        FF0 = len(LAYERS) * NT
        LG = len(LAYERS) * G

        with nc.Block() as block:
            @block.sync
            def _(sp):
                load_pieces(sp, sa, todo, raw_in)
                for g in range(G):
                    sp.wait_ge(sa["residual"], FF0 + GT * (g + 1))
                    sp.dma_start(x_mid[GT * g:GT * (g + 1)].rearrange("t p d -> p t d"),
                                 X[:, GT * g:GT * (g + 1), :]).then_inc(sa["stored"], 16)
                sp.wait_ge(sa["stored"], 16 * G)

            @block.gpsimd
            def _(pool):
                inverse_root(pool, sa, 0)
                for n in range(LG):
                    inverse_root(pool, sa, n + 1)
                    if n * CW < L0_AT:
                        for k in (2 * n, 2 * n + 1):
                            split_piece(pool, sa, raw_in, k, todo[k])
                pool.wait_ge(sa["products"], FF0)
                for k in range(2 * L0_AT // CW, len(todo)):
                    split_piece(pool, sa, raw_in, k, todo[k])
                for n in range(LG + 1, LG + G):
                    inverse_root(pool, sa, n)

            @block.tensor
            def _(pe):
                for t in range(GT):
                    transpose(pe, sa, t, t, XN[:, t % 2, :], None)
                for layer, w in enumerate(LAYERS):
                    m0 = layer * NT
                    if layer == 0:
                        linear_pe(pe, sa, 0, w)
                    with pe.Fori(int(layer == 0), G) as g:
                        linear_pe(pe, sa, g * GT + m0, w)
                with pe.Fori(0, G - 1) as g:
                    ffn_pe(pe, sa, g * GT + FF0, g, g * GT + (FF0 + GT), True)
                ffn_pe(pe, sa, FF0 + NT - GT, G - 1, 0, False)

            @block.scalar
            def _(act):
                for t in range(GT):
                    normalise(act, sa, t, 0, t, X[:, t, :], XN[:, t % 2, :], t >= 2)
                    high_half(act, sa, t, t, xt(XTH, t))
                for layer, w in enumerate(LAYERS):
                    m0 = layer * NT
                    with act.Fori(0, G) as g:
                        linear_act(act, sa, g * GT + m0, g + G * layer, (g + 1) % G * GT)
                with act.Fori(0, G - 1) as g:
                    ffn_act(act, sa, g * GT + FF0, g, g * GT + (FF0 + GT), g + (LG + 1), g * GT + GT, True)
                ffn_act(act, sa, FF0 + NT - GT, G - 1, 0, 0, 0, False)

            @block.vector
            def _(dve):
                dve.wait_ge(setup_done, 3)
                dve.wait_ge(x_loaded[0], 16)
                nc.vector.memset(minus_half[:, :], -0.5).then_inc(sa["consts"], 1)
                dve.wait_ge(sa["consts"], 1)
                moments(dve, sa, 0, [X[:, t, :] for t in range(GT)])
                offsets(dve, sa, 0)
                dve.wait_ge(x_loaded[1], 16)
                moments(dve, sa, 1, [X[:, GT + t, :] for t in range(GT)])
                for t in range(GT):
                    low_half(dve, sa, t, t, xt(XTL, t), xt(XTH, t))
                for g in range(2, G):
                    dve.wait_ge(x_loaded[g], 16)
                for layer, w in enumerate(LAYERS):
                    m0, last = layer * NT, layer == len(LAYERS) - 1
                    bias_at = None if w else (layer // 2) * NT
                    with dve.Fori(0, G - int(last)) as g:
                        linear_dve(dve, sa, g * GT + m0, g + G * layer, g * GT, (g + 2) % G * GT,
                                   None if bias_at is None else g * GT + bias_at)
                    if last:
                        linear_dve(dve, sa, m0 + NT - GT, G * layer + G - 1, NT - GT, None, bias_at + NT - GT)
                with dve.Fori(0, G - 1) as g:
                    ffn_dve(dve, sa, g * GT + FF0, g, g * GT + (FF0 + GT), g + (LG + 1), g * GT, g * GT + GT, True,
                            g * GT + (FF0 + 2 * GT - NT))
                ffn_dve(dve, sa, FF0 + NT - GT, G - 1, 0, 0, NT - GT, 0, False, 0)

        sb = dense_sems("b_", NORM)
        sp1 = dict((n, sem("p_" + n)) for n in (
            "w_loaded", "wd_high", "wd_low", "up_high", "up_low", "c_ps", "k_ps", "c_high", "c_low", "k_high", "k_low",
            "k_again", "ex_ps", "ex_high", "ex_low", "v_copied"))
        x_in = [sem(f"x_in{n}") for n in range(2)]
        ex_stored = [sem(f"ex_stored{n}") for n in range(4)]
        NEX = 2 * DC
        NOUT = NEX + GT

        NSLOT = 4

        def all_stored(eng):
            for n in range(NSLOT):
                eng.wait_ge(ex_stored[n], 16 * 3 * NEX * G // NSLOT)

        def ex_bank(n):
            return bank((2 + n) % 4)

        def k_again(pool, g):
            at = slice(GW * g, GW * (g + 1))
            pool.wait_ge(sp1["k_high"], g + 1)
            nc.gpsimd.tensor_scalar(K1[0:ROPE, 1, at], K1[0:ROPE, 0, at], 1.0, 1.0, ALU.mult,
                                    ALU.mult).then_inc(sp1["k_again"], 1)

        def project_pool(pool):
            for g in range(G):
                inverse_root(pool, sb, g)
                if g > 0:
                    k_again(pool, g - 1)
            k_again(pool, G - 1)

        def project_sync(sp):
            def load_x(g):
                if g >= 2:
                    sp.wait_ge(sb["normed"], GT * (g - 1))
                sp.dma_start(b_x[:, g % 2, :, :], x_mid[GT * g:GT * (g + 1)].rearrange("t p d -> p t d")
                             ).then_inc(x_in[g % 2], 16)

            load_x(0)
            for dst, src in [(b_wd, wdown)] + [(b_up[n][r:r + ROPE, :], w) for n, w in enumerate((wqu, wku, wvu))
                                               for r in (0, ROPE)]:
                sp.dma_start(dst, src).then_inc(sp1["w_loaded"], 16)
            load_x(1)
            for g in range(G):
                if g + 2 < G:
                    load_x(g + 2)
                for n in range(NEX):
                    c, eh, el = n % DC, b_eh[:, n % NSLOT, :], b_el[:, n % NSLOT, :]
                    ex, rows = (exq, ((0, eh), (1, eh), (2, el))) if n < DC else (exk, ((0, eh), (2, eh), (1, el)))
                    for r, src in rows:
                        sp.wait_ge(sp1["ex_high" if src is eh else "ex_low"], NEX * g + n + 1)
                        sp.dma_start(ex[32 * c:32 * (c + 1), HD * r:HD * (r + 1), GW * g:GW * (g + 1)],
                                     src.bitcast(F32)).then_inc(ex_stored[n % NSLOT], 16)
            all_stored(sp)

        def project_dve(dve):
            def x_moments(g):
                dve.wait_ge(x_in[g % 2], 16 * (g // 2 + 1))
                moments(dve, sb, g, [b_x[:, g % 2, t, :] for t in range(GT)])

            def x_low(n):
                low_half(dve, sb, n, n % GT, XAL[:, :, P * n:P * (n + 1)], XAH[:, :, P * n:P * (n + 1)])

            x_moments(0)
            offsets(dve, sb, 0)
            dve.wait_ge(sp1["wd_high"], 1)
            nc.vector.tensor_tensor(b_wdl[:, :, :], b_wd.rearrange("p (c n) -> p c n", c=DC), b_wdh[:, :, :],
                                    ALU.subtract).then_inc(sp1["wd_low"], 1)
            for n in range(3):
                dve.wait_ge(sp1["up_high"], n + 1)
                nc.vector.tensor_tensor(b_upl[n], b_up[n], b_uph[n], ALU.subtract).then_inc(sp1["up_low"], 1)
            x_moments(1)
            for n in range(GT):
                x_low(n)
            for g in range(G):
                dve.wait_ge(sp1["c_high"], 2 * g + 1)
                nc.vector.tensor_tensor(b_cq[ROPE:P, :], bank(0)[0:ROPE, :], b_cq[0:ROPE, :],
                                        ALU.subtract).then_inc(sp1["c_low"], 1)
                dve.wait_ge(sp1["c_high"], 2 * g + 2)
                nc.vector.tensor_tensor(b_ckv[0:ROPE, :], bank(0)[ROPE:P, :], b_ckv[ROPE:P, :],
                                        ALU.subtract).then_inc(sp1["c_low"], 1)
                dve.wait_ge(sp1["k_high"], g + 1)
                nc.vector.tensor_tensor(K2[ROPE:P, GW * g:GW * (g + 1)], bank(1)[ROPE:P, :], b_kt[ROPE:P, :],
                                        ALU.subtract).then_inc(sp1["k_low"], 1)
                if g + 1 < G:
                    dve.wait_ge(sb["normed"], GT * (g + 1))
                    offsets(dve, sb, g + 1)
                for n in range(NEX):
                    k = NEX * g + n
                    dve.wait_ge(sp1["ex_high"], k + 1)
                    if k >= NSLOT:
                        dve.wait_ge(ex_stored[n % NSLOT], 48 * (k // NSLOT))
                    nc.vector.tensor_tensor(b_el[:, n % NSLOT, :], ex_bank(n), b_eh[:, n % NSLOT, :],
                                            ALU.subtract).then_inc(sp1["ex_low"], 1)
                    if n % 2 and g + 1 < G:
                        x_low(GT * (g + 1) + n // 2)
                if g + 2 < G:
                    x_moments(g + 2)

        def project_act(act):
            def x_normalise(n):
                normalise(act, sb, n, n // GT, n % GT, b_x[:, n // GT % 2, n % GT, :], b_xn[:, n % 2, :], n >= 2)

            def x_high(n):
                high_half(act, sb, n, n % GT, XAH[:, :, P * n:P * (n + 1)])

            act.wait_ge(sp1["w_loaded"], 16 * 7)
            nc.scalar.copy(b_wdh[:, :, :], b_wd.rearrange("p (c n) -> p c n", c=DC)).then_inc(sp1["wd_high"], 1)
            for n in range(GT):
                x_normalise(n)
                x_high(n)
            for n in range(3):
                nc.scalar.copy(b_uph[n], b_up[n]).then_inc(sp1["up_high"], 1)
            for g in range(G):
                at = slice(GW * g, GW * (g + 1))
                act.wait_ge(sp1["c_ps"], g + 1)
                if g > 0:
                    act.wait_ge(sp1["ex_ps"], NOUT * g)
                nc.scalar.copy(b_cq[0:ROPE, :], bank(0)[0:ROPE, :]).then_inc(sp1["c_high"], 1)
                nc.scalar.copy(b_ckv[ROPE:P, :], bank(0)[ROPE:P, :]).then_inc(sp1["c_high"], 1)
                act.wait_ge(sp1["k_ps"], g + 1)
                if g > 0:
                    act.wait_ge(sp1["k_low"], g)
                nc.scalar.copy(b_kt[ROPE:P, :], bank(1)[ROPE:P, :])
                nc.scalar.copy(K2[0:ROPE, at], bank(1)[0:ROPE, :])
                nc.scalar.copy(K1[0:ROPE, 0, at], bank(1)[0:ROPE, :]).then_inc(sp1["k_high"], 1)
                for n in range(NEX):
                    k = NEX * g + n
                    act.wait_ge(sp1["ex_ps"], NOUT * g + n + 1)
                    if k >= NSLOT:
                        act.wait_ge(ex_stored[n % NSLOT], 48 * (k // NSLOT))
                    nc.scalar.copy(b_eh[:, n % NSLOT, :], ex_bank(n)).then_inc(sp1["ex_high"], 1)
                    if g + 1 < G:
                        if n % 2:
                            x_high(GT * (g + 1) + n // 2)
                        else:
                            x_normalise(GT * (g + 1) + n // 2)
                for t in range(GT):
                    act.wait_ge(sp1["ex_ps"], NOUT * g + NEX + t + 1)
                    nc.scalar.copy(VA[:, GT * g + t, :], ex_bank(NEX + t)).then_inc(sp1["v_copied"], 1)

        def project_pe(pe):
            def x_transpose(n):
                transpose(pe, sb, n, n % GT, b_xn[:, n % 2, :], n - 3 if n >= GT else None)

            for n in range(GT):
                x_transpose(n)
            for g in range(G):
                at = slice(GW * g, GW * (g + 1))
                pe.wait_ge(sb["low"], GT * (g + 1))
                pe.wait_ge(sp1["wd_low"], 1)
                if g > 0:
                    pe.wait_ge(sp1["v_copied"], GT * g)
                for k, signal in ((0, "c_ps"), (1, "k_ps")):
                    for c in range(DC):
                        last = split_products(nc, bank(k), b_wdh[:, c, P * k:P * (k + 1)],
                                              b_wdl[:, c, P * k:P * (k + 1)], XAH[:, c, at], XAL[:, c, at],
                                              c == 0, c == DC - 1)
                    last.then_inc(sp1[signal], 1)
                pe.wait_ge(sp1["up_low"], 3)
                for n in range(NOUT):
                    if n == 0:
                        pe.wait_ge(sp1["c_low"], 2 * g + 1)
                    if n == 2:
                        pe.wait_ge(sp1["c_low"], 2 * g + 2)
                        pe.wait_ge(sp1["k_low"], g + 1)
                    if n >= NSLOT:
                        pe.wait_ge(sp1["ex_low"], NEX * g + n - NSLOT + 1)
                    elif g > 0 and n < 2:
                        pe.wait_ge(sp1["v_copied"], GT * (g - 1) + n + 1)
                    part, c = n // DC, n % DC
                    both = b_ckv if part else b_cq
                    for up in (b_uph, b_upl):
                        if part < 2:
                            w, r = up[part][:, P * c:P * (c + 1)], both
                        else:
                            w, r = both[:, P * c:P * (c + 1)], up[part]
                        last = nc.tensor.matmul(ex_bank(n), w, r, start=up is b_uph, stop=up is b_upl)
                    last.then_inc(sp1["ex_ps"], 1)
                    if n % 2 and n < NEX and g + 1 < G:
                        x_transpose(GT * (g + 1) + n // 2)

        m = dict((n, sem("m_" + n)) for n in (
            "ones", "vst_init", "wraw_loaded", "wr_high", "wr_low", "q_ps", "q_high1", "q_high", "q_low", "mx_ps", "maxed", "max_t",
            "neg_max", "waited", "scores", "exps", "vst", "pv", "pv_out"))
        ex_in = [sem(f"m_ex_in{n}") for n in range(G)]
        row_in = [sem(f"m_row_in{n}") for n in range(2)]
        sums_out = [sem(f"m_sums_out{n}") for n in range(G)]
        TURN = 8
        TURNS = UNITS // TURN
        ST = (psum[:, 0:1024], psum[:, 1024:2048])
        MX = (bank(4), bank(5))
        QR = bank(6)
        AUX = bank(7)
        PVO, TR = AUX[:, 0:S], AUX[0:8, S:S + P]

        def active(i, k, lag):
            return not isinstance(i, int) or 0 <= TURN * i + k - lag < UNITS

        def count(i, k, lag, per, off):
            return i * (TURN * per) + (per * (k - lag) + off)

        def wait_unit(eng, s, i, k, lag, per, off):
            if active(i, k, lag):
                eng.wait_ge(s, count(i, k, lag, per, off))

        def wait_dma(eng, sems, i, k, lag, per):
            n = len(sems)
            if active(i, k, lag):
                eng.wait_ge(sems[(k - lag) % n], i * (TURN // n * per) + ((k - lag) // n + 1) * per)

        def steps(eng, step):
            for k in range(TURN):
                step(eng, 0, k)
            with eng.Fori(1, TURNS - 1) as i:
                for k in range(TURN):
                    step(eng, i, k)
            for k in range(TURN):
                step(eng, TURNS - 1, k)
            for k in range(4):
                step(eng, TURNS, k)

        def more_pairs(i, k):
            return not (isinstance(i, int) and i == TURNS - 1 and k >= G)

        def sync_step(sp, i, k):
            tg, pair = k % G, i * 2 + k // G
            if active(i, k, 0):
                if tg == 0 and more_pairs(i, k):
                    sp.wait_ge(m["wr_low"], i * 2 + (k // G + 1))
                    sp.dma_start(WRAW[:, (k // G + 1) % 2, :], wrope[bass.ds(i * 2 + (k // G + 1), 1)].rearrange(
                        "a p n -> p (a n)")).then_inc(m["wraw_loaded"], 16)
                wait_unit(sp, m["scores"], i, k, 4, 2, 2)
                cols = slice(GW * tg, GW * (tg + 1))
                sp.dma_start(X1[ROPE:KROW, tg, :, :].bitcast(F32),
                             exq[bass.ds(pair * 2, 2), :, cols].rearrange("h r t -> r h t")
                             ).then_inc(ex_in[tg], 16)
                sp.dma_start(K1[ROPE:KROW, :, cols].bitcast(F32),
                             exk[bass.ds(pair * 2, 2), :, cols].rearrange("h r t -> r h t")
                             ).then_inc(ex_in[tg], 16)
            if active(i, k, 2):
                wait_unit(sp, m["neg_max"], i, k, 2, 1, 1)
                for h in range(2):
                    sp.dma_start(X1[KROW:KROW + 1, (k - 2) % G, h, :].bitcast(F32), NM[4 * h:4 * h + 4, k % 2, :].bitcast(F32)
                                 ).then_inc(row_in[k % 2], 16)
            if active(i, k, 4):
                wait_unit(sp, m["pv_out"], i, k, 4, 1, 1)
                p4, t4 = (i * 2 + (k - 4) // G), (k - 4) % G
                for j in range(4):
                    h, b = j // 2, j % 2
                    c0 = GW * t4 + S * b
                    sp.dma_start(att[bass.ds(p4 * 2 + h, 1), :, c0:c0 + S],
                                 OSB[32 * j:32 * j + HD + 1, k % G, :]).then_inc(sums_out[k % G], 16)

        def pool_step(pool, i, k):
            tg = k % G
            if active(i, k, 0):
                pair = i * 2 + k // G
                wait_unit(pool, m["pv"], i, k, 4, 1, 1)
                nc.gpsimd.tensor_copy(VST[:, GT * tg:GT * (tg + 1), :, 0:HD],
                                      VA[:, GT * tg:GT * (tg + 1), bass.ds(pair * 8, 8)].rearrange(
                                          "p t (h d) -> p t h d", h=2)).then_inc(m["vst"], 1)
                if tg == 0 and more_pairs(i, k):
                    w = (k // G + 1) % 2
                    n = i * 2 + (k // G + 1)
                    split_rope(pool, i, k, w, n)

        def split_rope(pool, i, k, w, n):
            pool.wait_ge(m["wraw_loaded"], (n + 1) * 16)
            if not isinstance(i, int) or TURN * i + k > 0:
                pool.wait_ge(m["q_ps"], count(i, k, 0, 1, 0))
            pool.sem_inc(m["waited"], 1)
            nc.gpsimd.tensor_scalar(WRH[:, w, :], WRAW[:, w, :], 1.0, 1.0, ALU.mult,
                                    ALU.mult).then_inc(m["wr_high"], 1)
            pool.wait_ge(m["wr_high"], n + 1)
            nc.gpsimd.tensor_tensor(WRL[:, w, :], WRAW[:, w, :], WRH[:, w, :], ALU.subtract).then_inc(m["wr_low"], 1)

        def pe_step(pe, i, k):
            tg, w = k % G, k // G

            def maxima(j):
                h, b = j // 2, j % 2
                if j >= 2 or not (isinstance(i, int) and i * TURN + k - 1 == 0):
                    pe.wait_ge(m["maxed"], count(i, k, 1, 4, j - 1))
                t1 = (k - 1) % G
                for q in range(2):
                    last = nc.tensor.matmul(MX[j % 2][:, S * q:S * (q + 1)],
                                            X1[0:KM, t1, h, S * b + P * q:S * b + P * (q + 1)],
                                            K1[0:KM, h, GW * t1 + S * b:GW * t1 + S * (b + 1)], start=True, stop=True)
                last.then_inc(m["mx_ps"], 1)

            def queries(cs):
                for c in cs:
                    a = P * c
                    last = split_products(nc, QR, WRH[:, w, a:a + P], WRL[:, w, a:a + P],
                                          XAH[:, c, GW * tg:GW * (tg + 1)], XAL[:, c, GW * tg:GW * (tg + 1)], c == 0,
                                          c == DC - 1)
                return last

            if active(i, k, 1):
                wait_unit(pe, m["q_high"], i, k, 1, 1, 1)
                wait_dma(pe, ex_in, i, k, 1, 32)
                maxima(0)
                maxima(1)
            if active(i, k, 0):
                if tg == 0:
                    pe.wait_ge(m["wr_low"], i * 2 + (w + 1))
                wait_unit(pe, m["q_low"], i, k, 1, 1, 1)
                queries((0, 1))
            if active(i, k, 1):
                maxima(2)
                maxima(3)
            if active(i, k, 2):
                wait_unit(pe, m["maxed"], i, k, 2, 4, 4)
                wait_unit(pe, m["pv_out"], i, k, 5, 1, 1)
                wait_unit(pe, m["neg_max"], i, k, 3, 1, 1)
                nc.tensor.transpose(TR, MXS[:, k % 2, :], ident[:, :]).then_inc(m["max_t"], 1)
            if active(i, k, 0):
                queries((2, 3)).then_inc(m["q_ps"], 1)
            if active(i, k, 3):
                t3 = (k - 3) % G
                wait_dma(pe, row_in, i, k, 3, 32)
                wait_unit(pe, m["q_low"], i, k, 3, 1, 1)
                for h in range(2):
                    wait_unit(pe, m["exps"], i, k, 4, 2, h + 1)
                    for b in range(2):
                        for kt in range(2):
                            o = ST[h][:, 512 * b + S * kt:512 * b + S * (kt + 1)]
                            ks = slice(GW * t3 + S * b + P * kt, GW * t3 + S * b + P * (kt + 1))
                            qs = slice(S * b, S * (b + 1))
                            nc.tensor.matmul(o, K1[0:KROW + 1, h, ks], X1[0:KROW + 1, t3, h, qs], start=True,
                                             stop=False)
                            last = nc.tensor.matmul(o, K2[:, ks], X2[:, t3, h, qs], start=False, stop=True)
                    last.then_inc(m["scores"], 1)
            if active(i, k, 4):
                t4 = (k - 4) % G
                wait_unit(pe, m["exps"], i, k, 4, 2, 2)
                wait_unit(pe, m["vst"], i, k, 4, 1, 1)
                wait_unit(pe, m["neg_max"], i, k, 2, 1, 1)
                wait_unit(pe, m["pv_out"], i, k, 5, 1, 1)
                for kt in range(2):
                    for j in range(4):
                        h, b = j // 2, j % 2
                        last = nc.tensor.matmul(PVO[32 * j:32 * (j + 1), :], VST[:, GT * t4 + 2 * b + kt, h, :],
                                                PB[:, k % 2, 512 * j + S * kt:512 * j + S * (kt + 1)], start=(kt == 0),
                                                stop=(kt == 1))
                last.then_inc(m["pv"], 1)

        def act_step(act, i, k):
            tg = k % G
            if active(i, k, 2):
                wait_unit(act, m["max_t"], i, k, 2, 1, 1)
                wait_dma(act, row_in, i, k, 4, 32)
                nc.scalar.mul(NM[:, k % 2, :], TR, -1.0).then_inc(m["neg_max"], 1)
            if active(i, k, 0):
                wait_unit(act, m["q_ps"], i, k, 0, 1, 1)
                wait_unit(act, m["scores"], i, k, 4, 2, 2)
                nc.scalar.copy(X1[0:ROPE, tg, 0, :], QR[0:ROPE, :])
                nc.scalar.copy(X2[ROPE:P, tg, 0, :], QR[0:ROPE, :]).then_inc(m["q_high1"], 1)
                nc.scalar.copy(X1[0:ROPE, tg, 1, :], QR[ROPE:P, :])
                nc.scalar.copy(X2[ROPE:P, tg, 1, :], QR[ROPE:P, :]).then_inc(m["q_high"], 1)
            if active(i, k, 3):
                for h in range(2):
                    wait_unit(act, m["scores"], i, k, 3, 2, h + 1)
                    wait_unit(act, m["pv"], i, k, 5, 1, 1)
                    nc.scalar.activation(PB[:, (k - 3) % 2, 1024 * h:1024 * (h + 1)], ST[h], ACT.Exp,
                                         scale=SC).then_inc(m["exps"], 1)

        def dve_step(dve, i, k):
            tg = k % G
            if active(i, k, 1):
                wait_unit(dve, m["max_t"], i, k, 3, 1, 1)
                for j in range(4):
                    wait_unit(dve, m["mx_ps"], i, k, 1, 4, j + 1)
                    nc.vector.tensor_reduce(MXS[:, (k - 1) % 2, 2 * j:2 * j + 2],
                                            MX[j % 2].rearrange("p (q n) -> p q n", q=2), AXX,
                                            ALU.max).then_inc(m["maxed"], 1)
            if active(i, k, 0):
                wait_unit(dve, m["q_high1"], i, k, 0, 1, 1)
                nc.vector.tensor_tensor(X2[0:ROPE, tg, 0, :], QR[0:ROPE, :], X1[0:ROPE, tg, 0, :], ALU.subtract)
                wait_unit(dve, m["q_high"], i, k, 0, 1, 1)
                nc.vector.tensor_tensor(X2[0:ROPE, tg, 1, :], QR[ROPE:P, :], X2[ROPE:P, tg, 1, :],
                                        ALU.subtract).then_inc(m["q_low"], 1)
            if active(i, k, 4):
                wait_unit(dve, m["pv"], i, k, 4, 1, 1)
                wait_dma(dve, sums_out, i, k, 8, 64)
                nc.vector.tensor_copy(OSB[:, k % G, :], PVO).then_inc(m["pv_out"], 1)

        with nc.Block() as block:
            @block.sync
            def _(sp):
                sp.dma_start(WRAW[:, 0, :], wrope[0]).then_inc(m["wraw_loaded"], 16)
                project_sync(sp)
                sp.wait_ge(m["ones"], 1)
                steps(sp, sync_step)
                for n in range(G):
                    sp.wait_ge(sums_out[n], 64 * UNITS // G)

            @block.gpsimd
            def _(pool):
                split_rope(pool, 0, 0, 0, 0)
                project_pool(pool)
                pool.wait_ge(sp1["wd_low"], 1)
                nc.gpsimd.memset(VST[:, :, :, :], 0.0).then_inc(m["vst_init"], 1)
                pool.wait_ge(m["vst_init"], 1)
                nc.gpsimd.memset(VST[:, :, :, HD:HD + 1], 1.0).then_inc(m["vst_init"], 1)
                pool.wait_ge(m["vst_init"], 2)
                pool.wait_ge(sp1["v_copied"], NT)
                steps(pool, pool_step)

            @block.vector
            def _(dve):
                nc.vector.memset(K1[ROPE:96, :, :].bitcast(F32), 1.0).then_inc(m["ones"], 1)
                project_dve(dve)
                steps(dve, dve_step)

            @block.scalar
            def _(act):
                project_act(act)
                all_stored(act)
                steps(act, act_step)

            @block.tensor
            def _(pe):
                project_pe(pe)
                pe.wait_ge(sp1["v_copied"], NT)
                pe.wait_ge(sp1["ex_low"], NEX * G)
                pe.wait_ge(sb["low"], NT)
                pe.wait_ge(sp1["k_again"], G)
                steps(pe, pe_step)

        sc = dense_sems("c_", NORM + FFN + ("loaded",))
        craw_in = [sem(f"c_raw_in{n}") for n in range(2)]
        wo_cols = [(0, PW), (PW, 2 * PW), (2 * PW, DC * D)]
        ctodo = [(wo[:, a:b], L0_AT + a, b - a, None) for a, b in wo_cols]
        NWO = len(ctodo)
        ctodo += [p for i in range(NI) for p in pieces(i)]
        NUM = (XN[:, 0, :], XN[:, 1, :], SG[:, :])
        DEN = (bias_half[:, :], HF[:, :])
        o = dict((n, sem("o_" + n)) for n in ("zeros", "spread", "recip", "factor", "quotient"))
        num_in = [sem(f"o_num_in{n}") for n in range(3)]
        den_in = [sem(f"o_den_in{n}") for n in range(2)]

        def ot(W, Z, g):
            return Z[:, :, :] if g % 2 == 0 else half(W, 1).rearrange("p (c n) -> p c n", c=DC)

        with nc.Block() as block:
            @block.sync
            def _(sp):
                load_pieces(sp, sc, ctodo, craw_in)
                for g in range(G):
                    sp.wait_ge(sc["residual"], NT + GT * (g + 1))
                    sp.dma_start(out[GT * g:GT * (g + 1)].rearrange("t p d -> p t d"),
                                 X[:, GT * g:GT * (g + 1), :]).then_inc(sc["stored"], 16)
                sp.wait_ge(sc["stored"], 16 * G)

            @block.gpsimd
            def _(pool):
                nc.gpsimd.memset(spread[:, :, :], 0.0).then_inc(o["zeros"], 1)
                pool.wait_ge(o["zeros"], 1)
                for c in range(DC):
                    v = spread[:, c, :].rearrange("p (h d) -> p h d", d=HD)
                    nc.gpsimd.affine_select(out=v, in_=v, compare_op=ALU.not_equal, fill=1.0, base=-c * P // HD,
                                            pattern=[[-1, P // HD], [0, HD]],
                                            channel_multiplier=1).then_inc(o["spread"], 1)
                for k, piece in enumerate(ctodo):
                    if k == NWO + 12:
                        inverse_root(pool, sc, 0)
                    if k == NWO + 2 * L0_AT // CW:
                        pool.wait_ge(sc["products"], NT)
                    split_piece(pool, sc, craw_in, k, piece)
                for n in range(1, G):
                    inverse_root(pool, sc, n)

            @block.tensor
            def _(pe):
                def factors(g):
                    pe.wait_ge(o["recip"], g + 1)
                    for c in range(DC):
                        n = DC * g + c
                        if n >= GT:
                            pe.wait_ge(o["quotient"], n - GT + 1)
                        nc.tensor.matmul(bank(4 + c), spread[:, c, :], DEN[g % 2], start=True,
                                         stop=True).then_inc(o["factor"], 1)

                pe.wait_ge(o["spread"], DC)
                factors(0)
                for g in range(G):
                    if g + 1 < G:
                        factors(g + 1)
                    for t in range(GT):
                        if g > 0:
                            pe.wait_ge(sc["residual"], GT * (g - 1) + t + 1)
                        for c in range(DC):
                            if t == 0:
                                pe.wait_ge(sc["low"], DC * g + c + 1)
                                if g == 0:
                                    pe.wait_ge(sc["raw_read"], -(-D * (c + 1) // PW))
                            wh, wl = (half(W, 0)[:, D * c:D * (c + 1)] for W in (WH, WL))
                            last = split_products(nc, bank(t), ot(WH, XTH, g)[:, c, P * t:P * (t + 1)],
                                                  ot(WL, XTL, g)[:, c, P * t:P * (t + 1)], wh, wl, c == 0,
                                                  c == DC - 1)
                        last.then_inc(sc["products"], 1)
                for t in range(GT):
                    transpose(pe, sc, t, t, XN[:, t % 2, :], None)
                with pe.Fori(0, G - 1) as g:
                    ffn_pe(pe, sc, g * GT + NT, g, g * GT + GT, True)
                ffn_pe(pe, sc, 2 * NT - GT, G - 1, 0, False)

            @block.scalar
            def _(act):
                def load_den(g):
                    if g >= 2:
                        act.wait_ge(o["factor"], DC * (g - 1))
                    act.dma_start(DEN[g % 2], att[:, HD, GW * g:GW * (g + 1)]).then_inc(den_in[g % 2], 16)

                def load_num(n):
                    g, c = n // DC, n % DC
                    if n >= 3:
                        act.wait_ge(sc["low"], n - 2)
                    act.dma_start(NUM[n % 3], att[32 * c:32 * (c + 1), 0:HD, GW * g:GW * (g + 1)]
                                  ).then_inc(num_in[n % 3], 16)

                load_den(0)
                for n in range(3):
                    load_num(n)
                load_den(1)
                for g in range(G):
                    act.dma_start(X[:, GT * g:GT * (g + 1), :], x_mid[GT * g:GT * (g + 1)].rearrange("t p d -> p t d")
                                  ).then_inc(sc["loaded"], 16)
                for n in range(G * DC):
                    g, c = n // DC, n % DC
                    if c == 0 and 1 <= g < G - 1:
                        load_den(g + 1)
                    act.wait_ge(o["quotient"], n + 1)
                    if g >= 2:
                        act.wait_ge(sc["products"], GT * (g - 1))
                    nc.scalar.copy(ot(WH, XTH, g)[:, c, :], NUM[n % 3]).then_inc(sc["high"], 1)
                    if 1 <= n and n + 2 < G * DC:
                        load_num(n + 2)
                for t in range(GT):
                    normalise(act, sc, t, 0, t, X[:, t, :], XN[:, t % 2, :], t >= 2)
                    high_half(act, sc, t, t, xt(XTH, t))
                with act.Fori(0, G - 1) as g:
                    ffn_act(act, sc, g * GT + NT, g, g * GT + GT, g + 1, g * GT + GT, True)
                ffn_act(act, sc, 2 * NT - GT, G - 1, 0, 0, 0, False)

            @block.vector
            def _(dve):
                def invert(g):
                    dve.wait_ge(den_in[g % 2], 16 * (g // 2 + 1))
                    nc.vector.reciprocal(DEN[g % 2], DEN[g % 2]).then_inc(o["recip"], 1)

                def add_projection(g, t):
                    dve.wait_ge(sc["products"], GT * g + t + 1)
                    residual(sc, t, GT * g, 1.0, sc["residual"])

                def divide(n):
                    dve.wait_ge(o["factor"], n + 1)
                    dve.wait_ge(num_in[n % 3], 16 * (n // 3 + 1))
                    nc.vector.tensor_tensor(NUM[n % 3], NUM[n % 3], bank(4 + n % DC),
                                            ALU.mult).then_inc(o["quotient"], 1)

                def quotient_low(n):
                    g, c = n // DC, n % DC
                    dve.wait_ge(sc["high"], n + 1)
                    if g >= 2:
                        dve.wait_ge(sc["products"], GT * (g - 1))
                    nc.vector.tensor_tensor(ot(WL, XTL, g)[:, c, :], NUM[n % 3], ot(WH, XTH, g)[:, c, :],
                                            ALU.subtract).then_inc(sc["low"], 1)

                invert(0)
                divide(0)
                for n in range(G * DC):
                    g, c = n // DC, n % DC
                    if n + 1 < G * DC:
                        divide(n + 1)
                    quotient_low(n)
                    if c == 1 and g + 1 < G:
                        invert(g + 1)
                    if n == DC:
                        dve.wait_ge(sc["loaded"], 16 * G)
                    if g > 0:
                        add_projection(g - 1, c)
                add_projection(G - 1, 0)
                add_projection(G - 1, 1)
                dve.wait_ge(sc["residual"], GT)
                moments(dve, sc, 0, [X[:, t, :] for t in range(GT)])
                offsets(dve, sc, 0)
                add_projection(G - 1, 2)
                add_projection(G - 1, 3)
                for t in range(GT):
                    low_half(dve, sc, NT + t, t, xt(XTL, t), xt(XTH, t))
                with dve.Fori(0, G - 1) as g:
                    ffn_dve(dve, sc, g * GT + NT, g, g * GT + GT, g + 1, g * GT, g * GT + GT, True, g * GT + 2 * GT)
                ffn_dve(dve, sc, 2 * NT - GT, G - 1, 0, 0, NT - GT, 0, False, 0)


_ORDER = ("x", "wT", "mwT", "maskT", "a_er", "b_er", "coef", "scal", "bias", "ffw", "wdown", "wqu", "wku", "wvu",
          "wrope", "wo")


def kernel(**inputs):
    import numpy as np
    import concourse.bacc as bacc
    from concourse.bass_utils import run_bass_kernel_spmd

    a = {k: np.asarray(v) for k, v in inputs.items()}
    data = a["L0_attn_data"]

    def rows(w):
        return np.ascontiguousarray(w.reshape(DC, P, -1).transpose(1, 0, 2).reshape(P, -1))

    gu, dn = a["L1_ffn_w_gate_up"], a["L1_ffn_w_down"]
    ffw = np.zeros((NI, P, CW), gu.dtype)
    for i in range(NI):
        n = min(P, I_FF - P * i)
        for k in range(2):
            w = gu[k * I_FF + P * i:k * I_FF + P * i + n].T.reshape(DC, P, n).transpose(1, 0, 2)
            ffw[i, :, k * D:(k + 1) * D].reshape(P, DC, P)[:, :, :n] = w
        ffw[i, :n, 2 * D:] = dn[:, P * i:P * i + n].T
    krope = a["L1_attn_Wk_rope"]
    wr = a["L1_attn_Wq_rope"].reshape(DC, P, NHP, P).transpose(2, 1, 0, 3).reshape(NHP, P, DC * P)
    laid = {
        "x": data.reshape(NT, P, D),
        "wT": rows(a["L0_ffn_W"].T),
        "mwT": rows(a["L0_attn_weight"].T),
        "maskT": rows(a["L0_attn_mask"].T),
        "a_er": a["L0_ffn_A"].reshape(2, P, D).transpose(1, 0, 2),
        "b_er": a["L0_ffn_Bf"].transpose(0, 2, 1).reshape(2, P, D).transpose(1, 0, 2),
        "coef": np.repeat(a["L0_ffn_coeffs"], 16).reshape(2, P).T,
        "scal": np.repeat(a["L0_ffn_scales"], 16).reshape(2, P).T,
        "bias": a["L0_ffn_bias"].reshape(1, D),
        "ffw": ffw,
        "wdown": rows(np.concatenate([a["L1_attn_Wq_down"], a["L1_attn_Wkv_down"], krope, krope], axis=1)),
        "wqu": a["L1_attn_Wq_up"],
        "wku": a["L1_attn_Wk_up"],
        "wvu": a["L1_attn_Wv_up"],
        "wrope": wr,
        "wo": rows(a["L1_attn_Wo"]),
    }
    nc = bacc.Bacc("TRN2", target_bir_lowering=False, num_devices=1)
    arrays, args = {}, []
    for name in _ORDER:
        v = np.ascontiguousarray(laid[name])
        arrays["in_" + name] = v
        args.append(nc.dram_tensor("in_" + name, v.shape, mybir.dt.from_np(v.dtype), kind="ExternalInput").ap())
    out = nc.dram_tensor("out", (NT, P, D), F32, kind="ExternalOutput").ap()
    build(nc, *args, out)
    got = run_bass_kernel_spmd(nc, [arrays], core_ids=[0]).results[0]["out"]
    return got.reshape(data.shape)
```
